# Optimizing a Trainium2 kernel written in Bass

```python
import numpy as np
import jax
import jax.numpy as jnp

def _softmax(x, axis=-1):
    return jax.nn.softmax(x, axis=axis)

def _gelu(x):
    return jax.nn.gelu(x, approximate=True)

def _silu(x):
    return jax.nn.silu(x)

def _sigmoid(x):
    return jax.nn.sigmoid(x)

def _layernorm(x, axis=-1, eps=1e-05):
    m = jnp.mean(x, axis=axis, keepdims=True)
    v = jnp.var(x, axis=axis, keepdims=True)
    return (x - m) / jnp.sqrt(v + eps)

def _scatter_add(tgt, idx, src, axis=0):
    return tgt.at[idx].add(src)

def _segment_sum(src, seg, n):
    return jax.ops.segment_sum(src, seg, n)
kernel_name = 'mk_adj_preln_d4_adj_r2_98d958'

def setup_inputs(seed: int=0):
    np.random.seed(seed)
    _w = jnp.asarray

    def _rec_inputs():
        import jax
        import jax.numpy as jnp
        _gk = jax.random.key(seed)
        x = 0.0001732 + 1 * jax.random.normal(jax.random.fold_in(_gk, 1), (5120, 64), jnp.float32)
        _a = jax.random.bernoulli(jax.random.fold_in(_gk, 2), 0.0015625, (5120, 5120))
        _af = _a.astype(jnp.float32)
        _af = _af * jax.random.uniform(jax.random.fold_in(_gk, 3), (5120, 5120), jnp.float32, 0.05, 0.02)
        adj = _af
        return (x, adj)
    x, adj = _rec_inputs()

    def _L0_gnn_setup():
        import jax, jax.numpy as jnp
        import numpy as np
        N_USERS = 2048
        N_ITEMS = 3072
        EMB = 64
        LN_EPS = 1e-05
        key = jax.random.key(seed)
        ks = jax.random.split(key, 10)
        N = N_USERS + N_ITEMS
        ego = jax.random.normal(ks[0], (N, EMB), jnp.float32)
        adj = (jax.random.uniform(ks[1], (N, N), jnp.float32) < 0.01).astype(jnp.float32) * 0.02
        xav = float(np.sqrt(6.0 / (EMB + EMB)))
        W_u = jax.random.uniform(ks[2], (EMB, EMB), jnp.float32, -xav, xav)
        W_i = jax.random.uniform(ks[3], (EMB, EMB), jnp.float32, -xav, xav)
        diag_u = jax.random.uniform(ks[4], (N_USERS,), jnp.float32, 0.99, 1.01)
        diag_i = jax.random.uniform(ks[5], (N_ITEMS,), jnp.float32, 0.99, 1.01)
        par_u = jax.random.uniform(ks[6], (2,), jnp.float32, 0.0, 0.99)
        par_i = jax.random.uniform(ks[7], (2,), jnp.float32, 0.0, 0.99)
        ln_gamma = jnp.ones((EMB,), jnp.float32)
        ln_beta = jnp.zeros((EMB,), jnp.float32)
        return {'ego_embeddings': ego, 'adj': adj, 'W_u': W_u, 'diag_u': diag_u, 'par_u': par_u, 'W_i': W_i, 'diag_i': diag_i, 'par_i': par_i, 'ln_gamma': ln_gamma, 'ln_beta': ln_beta}
    _L0_gnn_all = _L0_gnn_setup()
    _L0_gnn_in = {k: v for k, v in _L0_gnn_all.items() if k in ('W_u', 'diag_u', 'par_u', 'W_i', 'diag_i', 'par_i', 'ln_gamma', 'ln_beta')}
    del _L0_gnn_all

    def _L1_gnn_setup():
        import jax, jax.numpy as jnp
        import numpy as np
        N = 8192
        D = 64
        key = jax.random.key(seed)
        kx, ka = jax.random.split(key)
        x = jax.random.normal(kx, (N, D), dtype=jnp.float32)
        adj = jax.random.uniform(ka, (N, N), dtype=jnp.float32)
        return {'x': x, 'adj': adj}
    _L1_gnn_all = _L1_gnn_setup()
    _L1_gnn_in = {k: v for k, v in _L1_gnn_all.items() if k in ()}
    del _L1_gnn_all

    def _L2_gnn_setup():
        import jax, jax.numpy as jnp
        import numpy as np
        N, F_IN, F_OUT, K = (8192, 64, 64, 3)
        key = jax.random.key(seed)
        k1, k2, k3, k4 = jax.random.split(key, 4)
        x = jax.random.normal(k1, (N, F_IN), dtype=jnp.float32)
        L_tilde = jax.random.normal(k2, (N, N), dtype=jnp.float32) / np.float32(np.sqrt(N))
        stdv = 1.0 / np.sqrt(F_OUT)
        weights = jax.random.uniform(k3, (K + 1, F_IN, F_OUT), dtype=jnp.float32, minval=-stdv, maxval=stdv)
        bias = jax.random.uniform(k4, (F_OUT,), dtype=jnp.float32, minval=-stdv, maxval=stdv)
        return {'x': x, 'L_tilde': L_tilde, 'weights': weights, 'bias': bias}
    _L2_gnn_all = _L2_gnn_setup()
    _L2_gnn_in = {k: v for k, v in _L2_gnn_all.items() if k in ('weights', 'bias')}
    del _L2_gnn_all

    def _L3_gnn_setup():
        import jax, jax.numpy as jnp
        import numpy as np
        N = 5000
        DIN = 64
        DOUT = 64
        key = jax.random.key(seed)
        kx, ka, kw = jax.random.split(key, 3)
        x = jax.random.normal(kx, (N, DIN), dtype=jnp.float32)
        u = jax.random.uniform(ka, (N, N), dtype=jnp.float32)
        adj = (u < 0.01).astype(jnp.float32)
        adj = jnp.maximum(adj, adj.T) * (1.0 - jnp.eye(N, dtype=jnp.float32))
        W = jax.random.normal(kw, (DIN, DOUT), dtype=jnp.float32) * (1.0 / np.sqrt(DIN))
        b = jnp.zeros((DOUT,), dtype=jnp.float32)
        return {'x': x, 'adj_matrix': adj, 'W': W, 'b': b}
    _L3_gnn_all = _L3_gnn_setup()
    _L3_gnn_in = {k: v for k, v in _L3_gnn_all.items() if k in ('W', 'b')}
    del _L3_gnn_all
    return {'x': x, 'adj': adj, 'L0_gnn_W_u': _L0_gnn_in['W_u'], 'L0_gnn_diag_u': _L0_gnn_in['diag_u'], 'L0_gnn_par_u': _L0_gnn_in['par_u'], 'L0_gnn_W_i': _L0_gnn_in['W_i'], 'L0_gnn_diag_i': _L0_gnn_in['diag_i'], 'L0_gnn_par_i': _L0_gnn_in['par_i'], 'L0_gnn_ln_gamma': _L0_gnn_in['ln_gamma'], 'L0_gnn_ln_beta': _L0_gnn_in['ln_beta'], 'L2_gnn_weights': _L2_gnn_in['weights'], 'L2_gnn_bias': _L2_gnn_in['bias'], 'L3_gnn_W': _L3_gnn_in['W'], 'L3_gnn_b': _L3_gnn_in['b']}

def reference(x, adj, L0_gnn_W_u, L0_gnn_diag_u, L0_gnn_par_u, L0_gnn_W_i, L0_gnn_diag_i, L0_gnn_par_i, L0_gnn_ln_gamma, L0_gnn_ln_beta, L2_gnn_weights, L2_gnn_bias, L3_gnn_W, L3_gnn_b):
    import jax
    import jax.numpy as jnp

    def _L0_gnn_ref(ego_embeddings, adj, W_u, diag_u, par_u, W_i, diag_i, par_i, ln_gamma, ln_beta):
        import jax, jax.numpy as jnp
        import numpy as np
        N_USERS = 2048
        N_ITEMS = 3072
        EMB = 64
        LN_EPS = 1e-05
        nu = diag_u.shape[0]
        res = ego_embeddings
        ego_u = ego_embeddings[:nu]
        ego_i = ego_embeddings[nu:]
        u = par_u[0] * par_u[1] * (diag_u[:, None] * ego_u @ W_u) + ego_u
        i = par_i[0] * par_i[1] * (diag_i[:, None] * ego_i @ W_i) + ego_i
        e = jnp.concatenate([u, i], axis=0)
        h = adj @ (adj.T @ e)
        mu = jnp.mean(h, axis=-1, keepdims=True)
        var = jnp.var(h, axis=-1, keepdims=True)
        out = (h - mu) * jax.lax.rsqrt(var + LN_EPS) * ln_gamma + ln_beta + res
        return out

    def _L1_gnn_ref(x, adj):
        import jax, jax.numpy as jnp
        import numpy as np
        N = 8192
        D = 64
        return jnp.matmul(adj, x)

    def _L2_gnn_ref(x, L_tilde, weights, bias):
        import jax, jax.numpy as jnp
        import numpy as np
        N, F_IN, F_OUT, K = (8192, 64, 64, 3)
        T_prev = x
        out = T_prev @ weights[0]
        T_curr = L_tilde @ x
        out = out + T_curr @ weights[1]
        for k in range(2, K + 1):
            T_next = 2.0 * (L_tilde @ T_curr) - T_prev
            out = out + T_next @ weights[k]
            T_prev, T_curr = (T_curr, T_next)
        return out + bias

    def _L3_gnn_ref(x, adj_matrix, W, b):
        import jax, jax.numpy as jnp
        import numpy as np
        N = 5000
        DIN = 64
        DOUT = 64
        n = adj_matrix.shape[0]
        a = adj_matrix + jnp.eye(n, dtype=adj_matrix.dtype)
        degree = jnp.sum(a, axis=1)
        d_is = jnp.power(degree, -0.5)
        d_is = jnp.where(jnp.isinf(d_is), 0.0, d_is)
        a_norm = d_is[:, None] * a * d_is[None, :]
        h = x @ W + b
        out = jnp.maximum(a_norm @ h, 0.0)
        return out
    h = jnp.maximum(_layernorm(x, axis=-1), 0.0)
    x = x + _L0_gnn_ref(h, adj, L0_gnn_W_u, L0_gnn_diag_u, L0_gnn_par_u, L0_gnn_W_i, L0_gnn_diag_i, L0_gnn_par_i, L0_gnn_ln_gamma, L0_gnn_ln_beta)
    h = jnp.maximum(_layernorm(x, axis=-1), 0.0)
    x = x + _L1_gnn_ref(h, adj)
    h = jnp.maximum(_layernorm(x, axis=-1), 0.0)
    x = x + _L2_gnn_ref(h, adj, L2_gnn_weights, L2_gnn_bias)
    h = jnp.maximum(_layernorm(x, axis=-1), 0.0)
    x = x + _L3_gnn_ref(h, adj, L3_gnn_W, L3_gnn_b)
    return x

_drawn_inputs = setup_inputs


def setup_inputs(seed=0):
    import zlib

    import numpy as np

    out = dict(_drawn_inputs(seed))
    spreads = {'L0_gnn_ln_gamma': (1.0, 0.2), 'L0_gnn_ln_beta': (0.0, 0.1), 'L3_gnn_b': (0.0, 0.292)}
    factors = {'L0_gnn_diag_u': 8.0, 'L0_gnn_diag_i': 8.0}
    for name, (base, spread) in spreads.items():
        noise = np.random.default_rng([zlib.crc32(name.encode()), seed]).standard_normal(out[name].shape)
        drawn = base * np.exp(spread * noise) if base else spread * noise
        out[name] = jnp.asarray(drawn.astype(out[name].dtype))
    for name, factor in factors.items():
        out[name] = (out[name] * factor).astype(out[name].dtype)
    return out
```

```python
import concourse.bass as bass
from concourse import mybir
from contextlib import ExitStack
import numpy as np

F32 = mybir.dt.float32
F32R = mybir.dt.float32r
ALU = mybir.AluOpType
ACT = mybir.ActivationFunctionType
AX = mybir.AxisListType

P = 128
N = 5120
D = 64
U = 2048
B = 512
SUB = B // P
NB = N // B
NT = N // P
HALVES = 2
HS = SUB // HALVES
PASSES = 5
EPS = 1e-5
RD = SUB * D


class Chain:

    def __init__(self, eng, sem):
        self.eng, self.sem, self.n = eng, sem, 0

    def restart(self):
        self.eng.sem_clear(self.sem)
        self.n = 0

    def step(self, ins):
        ins.then_inc(self.sem, 1)
        self.n += 1
        self.eng.wait_ge(self.sem, self.n)


def feature_mean_scale(op, chain, v, centred, square, mean, rstd, minus_half, reduce_last):
    wide = list(v.shape)
    reduce_last(chain, v, square, mean)
    chain.step(op.tensor_scalar(mean, mean, 1.0 / D, None, ALU.mult))
    chain.step(op.tensor_tensor(centred, v, mean.unsqueeze(2).broadcast_to(wide), ALU.subtract))
    chain.step(op.tensor_tensor(square, centred, centred, ALU.mult))
    reduce_last(chain, square, square, rstd)
    chain.step(op.tensor_scalar(rstd, rstd, 1.0 / D, EPS, ALU.mult, ALU.add))


def gnn_stack(nc, x_d, adj_d, wu_d, du_d, pu_d, wi_d, di_d, pi_d, gam_d, bet_d, w2_d, b2_d, w3_d, b3_d, out_d):
    ctx = ExitStack()
    with ctx:
        def sb(name, shape, dt=F32):
            return ctx.enter_context(nc.sbuf_tensor(name, shape, dt))

        def sem(name):
            return ctx.enter_context(nc.semaphore(name))

        raw = sb("raw", [P, NB, SUB, B])
        high = sb("high", [P, 2, SUB, B], F32R)
        low = sb("low", [P, 2, SUB, B], F32R)
        with nc.sbuf_tensor("h_acc", [P, NB, B], F32) as h_acc:
            pass
        feats_b = sb("feats_b", [P, NT, 2 * D], F32R)
        feats_a = sb("feats_a", [P, NT, 2 * D], F32R)
        with nc.sbuf_tensor("S", [P, NT, D], F32) as S:
            pass
        row_tmp = sb("row_tmp", [P, 8, SUB, D])
        out_rows = sb("out_rows", [P, 2, SUB, D])
        X = sb("X", [P, NT, D])
        E = sb("E", [P, NT, D])
        R = sb("R", [P, NT, D])
        y_sb = sb("y_sb", [P, B])
        xt2 = [sb(f"xt{i}", [D, B]) for i in range(2)]
        xt_sb = xt2[0]
        t_cur = sb("t_cur", [P, SUB, 2 * D], F32R)
        deg_part = sb("deg_part", [P, NT, NB])
        dis = sb("dis", [P, NT])
        diag = sb("diag", [P, NT])
        par = sb("par", [P, 4])
        mean = sb("mean", [P, NT])
        rstd = sb("rstd", [P, NT])
        minus_half = sb("minus_half", [P, NT])
        gam = sb("gam", [P, D])
        bet = sb("bet", [P, D])
        b2 = sb("b2", [P, D])
        b3 = sb("b3", [P, D])
        w_in = sb("w_in", [D, 2, D])
        w2 = sb("w2", [D, 4, D])
        w3 = sb("w3", [D, D])
        ident = sb("ident", [P, P])
        fold = sb("fold", [P, D])

        turned = [ctx.enter_context(nc.psum_tensor(f"turned{h}", [P, HS, B], F32)) for h in range(HALVES)]
        acc = [ctx.enter_context(nc.psum_tensor(f"acc{i}", [P, B], F32)) for i in range(2)]
        aux = [ctx.enter_context(nc.psum_tensor(f"aux{i}", [P, B], F32)) for i in range(2)]

        raw_in = [sem(f"raw_in{s}") for s in range(NB)]
        consts_in = sem("consts_in")
        x_in = sem("x_in")
        made = sem("made")
        block_turned = sem("block_turned")
        high_ready = sem("high_ready")
        low_ready = sem("low_ready")
        half_used = sem("half_used")
        deg_summed = sem("deg_summed")
        h_added = sem("h_added")
        t_done = sem("t_done")
        t_saved = sem("t_saved")
        t_turned = sem("t_turned")
        t_high = sem("t_high")
        t_ready = sem("t_ready")
        ez_ready = sem("ez_ready")
        ez_turned = sem("ez_turned")
        ez_saved = sem("ez_saved")
        ez_mult = sem("ez_mult")
        e_ready = sem("e_ready")
        h_rows = sem("h_rows")
        h_rows_saved = sem("h_rows_saved")
        y_saved = sem("y_saved")
        y_rows = sem("y_rows")
        y_rows_saved = sem("y_rows_saved")
        feat_rows = sem("feat_rows")
        feat_turned = sem("feat_turned")
        feat_saved = sem("feat_saved")
        feat_mult = sem("feat_mult")
        feat_mult_saved = sem("feat_mult_saved")
        feats_ready = sem("feats_ready")
        deg_ready = sem("deg_ready")
        var_ready = sem("var_ready")
        pow_ready = sem("pow_ready")
        out_ready = sem("out_ready")
        out_stored = sem("out_stored")
        rows_taken = sem("rows_taken")
        dve_step = sem("dve_step")
        pe_held = sem("pe_held")
        pool_held = sem("pool_held")
        pool_step = sem("pool_step")

        adj_v = adj_d.rearrange("(m a p) (g k) -> p m a g k", a=SUB, p=P, k=B)
        x_v = x_d.rearrange("(t p) d -> p t d", p=P)
        out_v = out_d.rearrange("(m a p) d -> p m a d", a=SUB, p=P)
        y_nat = row_tmp[:, 0]
        wy_nat = row_tmp[:, 1]
        feat_row = row_tmp[:, 2]
        centred_row, square_row, x_row, gs_row = (row_tmp[:, i] for i in range(3, 7))

        FEATS = [feats_a, feats_b, feats_a, feats_b, feats_a]
        NEXT = [feats_b, feats_a, feats_b, feats_a, None]
        WEIGHTS = [(w2[:, 0, :],), (w2[:, 1, :],), (w2[:, 2, :],), (w2[:, 3, :], w3[:, :]), ()]
        W_BASE = [0, 10, 20, 30, 50]
        W_STEP = [((4, 5),), ((4, 5),), ((4, 5),), ((3, 4), (7, 8)), ()]
        CONST_LOADS = 16 * 12

        def tile_no(p, m, k):
            return NB * NB + NB * NB * p + NB * m + k

        block = ctx.enter_context(nc.Block())

        @block.sync
        def _(sp):
            sp.dma_start(X[:, :, :], x_v).then_inc(x_in, 16)
            for m in range(NB):
                sp.dma_start(raw[:, m], adj_v[:, m, :, 0, :]).then_inc(raw_in[m], 16)
            with sp.Fori(1, NB) as g:
                for m in range(NB):
                    sp.wait_ge(block_turned, 2 * (g * NB - NB + m + 1))
                    sp.wait_ge(deg_summed, g * NB - NB + m + 1)
                    sp.dma_start(raw[:, m], adj_v[:, m, :, bass.ds(g, 1), :].rearrange("p a g k -> p a (g k)")).then_inc(raw_in[m], 16)
            for k in range(NB):
                sp.wait_ge(block_turned, 2 * (NB * (NB - 1) + k + 1))
                sp.wait_ge(deg_summed, NB * (NB - 1) + k + 1)
                sp.dma_start(raw[:, k], adj_v[:, 0, :, k, :]).then_inc(raw_in[k], 16)
            for p in range(PASSES):
                with sp.Fori(1 if p == 0 else 0, NB) as m:
                    for k in range(NB):
                        sp.wait_ge(block_turned, (m * NB) * 2 + 2 * (tile_no(p, 0, k) - NB + 1))
                        sp.dma_start(raw[:, k], adj_v[:, bass.ds(m, 1), :, k, :].rearrange("p m a k -> p (m a) k")).then_inc(raw_in[k], 16)

        @block.tensor
        def _(pe):
            def turn(n, slot, loads):
                pe.wait_ge(raw_in[slot], loads * 16)
                for h in range(HALVES):
                    if not (isinstance(n, int) and n == 0):
                        pe.wait_ge(low_ready, n * 2 + (h - 1))
                    for b in range(HS):
                        for a in range(SUB):
                            last = nc.tensor.transpose(turned[h][:, b, a * P:(a + 1) * P],
                                                       raw[:, slot, a, (h * HS + b) * P:(h * HS + b + 1) * P], ident[:, :])
                    last.then_inc(block_turned, 1)

            def multiply(n, parity, feats, bank, start, stop):
                for h in range(HALVES):
                    pe.wait_ge(low_ready, n * 2 + (h + 1))
                    for b in range(HS):
                        i = h * HS + b
                        for part in (high, low):
                            last = nc.tensor.matmul(bank[:, :], feats[:, i, :], part[:, parity, i, :],
                                                    start=start and i == 0 and part is high,
                                                    stop=stop and i == SUB - 1 and part is low)
                    last.then_inc(half_used, 1)

            pe.wait_ge(made, 3)
            pe.wait_ge(consts_in, CONST_LOADS)
            pe.wait_ge(ez_ready, 1)
            for m in range(NB + 1):
                if m < NB:
                    if m >= 1:
                        pe.wait_ge(ez_saved, m)
                    for a in range(SUB):
                        last = nc.tensor.transpose(aux[0][0:D, a * P:(a + 1) * P], S[:, m * SUB + a, :], ident[:, :])
                    last.then_inc(ez_turned, 1)
                if m >= 1:
                    r = m - 1
                    pe.wait_ge(ez_saved, r + 1)
                    if r >= 1:
                        pe.wait_ge(e_ready, r)
                    w = w_in[:, 0 if r * B < U else 1, :]
                    for a in range(SUB):
                        last = nc.tensor.matmul(aux[1][:, a * D:(a + 1) * D], xt2[r % 2][:, a * P:(a + 1) * P], w,
                                                start=True, stop=True)
                    last.then_inc(ez_mult, 1)
            pe.wait_ge(e_ready, NB)

            def group(g, first):
                if not first:
                    pe.wait_ge(t_ready, g)
                for m in range(NB):
                    pe.wait_ge(raw_in[m], g * 16 + 16)
                    for a in range(SUB):
                        last = nc.tensor.matmul(aux[0][0:D, :], E[:, m * SUB + a, :], raw[:, m, a, :],
                                                start=(m == 0 and a == 0), stop=(m == NB - 1 and a == SUB - 1))
                last.then_inc(t_done, 1)
                turn(g * NB, 0, g + 1)
                pe.wait_ge(t_saved, g + 1)
                pe.sem_inc(pe_held, 1)
                for b in range(SUB):
                    last = nc.tensor.transpose(aux[1][:, b * D:(b + 1) * D], xt_sb[:, b * P:(b + 1) * P], ident[0:D, 0:D])
                last.then_inc(t_turned, 1)
                pe.wait_ge(t_ready, g + 1)
                for m in range(NB):
                    n = g * NB + m
                    if m + 1 < NB:
                        turn(n + 1, m + 1, g + 1)
                    if not (first and m < 2):
                        pe.wait_ge(h_added, n - 1)
                    multiply(n, m % 2, t_cur, acc[m % 2], True, True)

            group(0, True)
            with pe.Fori(1, NB) as g:
                group(g, False)

            pe.wait_ge(h_added, NB * NB)
            for m in range(NB):
                if m >= 2:
                    pe.wait_ge(h_rows_saved, m - 1)
                for a in range(SUB):
                    last = nc.tensor.matmul(aux[m % 2][:, a * D:(a + 1) * D], h_acc[:, m, a * P:(a + 1) * P], fold[:, :],
                                            start=True, stop=True)
                last.then_inc(h_rows, 1)

            def row(p, m, prev_p):
                first = isinstance(m, int)
                r = m + NB * p
                q = {} if prev_p is None else {j: W_BASE[prev_p] + len(WEIGHTS[prev_p]) * (NB - 1 if first else m - 1) + j
                                               for j in range(len(WEIGHTS[prev_p]))}
                for k in range(NB):
                    n = m * NB + tile_no(p, 0, k)
                    turn(n, k, m + (NB + 1 + NB * p))
                    if k == 0:
                        if prev_p is not None:
                            pe.wait_ge(feats_ready, NB * prev_p + NB)
                            multiply(n - 1, 1, FEATS[prev_p][:, (NB - 1) * SUB:NB * SUB], acc[0], False, True)
                        continue
                    if k == 1:
                        if prev_p is None:
                            pass
                        else:
                            pe.wait_ge(y_saved, r)
                    if first:
                        pe.wait_ge(feats_ready, NB * p + k)
                    multiply(n - 1, (k - 1) % 2, FEATS[p][:, (k - 1) * SUB:k * SUB], acc[0], k == 1, False)
                    if prev_p is None:
                        continue
                    if k == 1:
                        rows_out(r)
                    for j, (at_turn, at_mult) in enumerate(W_STEP[prev_p]):
                        if k == at_turn:
                            weigh_turn(q[j])
                        if k == at_mult:
                            weigh_mult(q[j], WEIGHTS[prev_p][j])

            def rows_out(r):
                pe.wait_ge(y_saved, r)
                if not (isinstance(r, int) and r < 2):
                    pe.wait_ge(rows_taken, r)
                for a in range(SUB):
                    last = nc.tensor.matmul(aux[0][:, a * D:(a + 1) * D], y_sb[:, a * P:(a + 1) * P], fold[:, :],
                                            start=True, stop=True)
                last.then_inc(y_rows, 1)

            def weigh_turn(q):
                pe.wait_ge(feat_rows, q + 1)
                pe.sem_inc(pe_held, 1)
                for a in range(SUB):
                    last = nc.tensor.transpose(aux[1][0:D, a * P:(a + 1) * P], feat_row[:, a, :], ident[:, :])
                last.then_inc(feat_turned, 1)

            def weigh_mult(q, w):
                pe.wait_ge(feat_saved, q + 1)
                for a in range(SUB):
                    last = nc.tensor.matmul(aux[0][:, RD + a * D:RD + (a + 1) * D], xt_sb[:, a * P:(a + 1) * P], w,
                                            start=True, stop=True)
                last.then_inc(feat_mult, 1)

            for p in range(PASSES):
                row(p, 0, p - 1 if p else None)
                with pe.Fori(1, NB) as m:
                    row(p, m, p)
            multiply(tile_no(PASSES, 0, 0) - 1, 1, FEATS[PASSES - 1][:, (NB - 1) * SUB:NB * SUB], acc[0], False, True)
            rows_out(NB * PASSES)

        @block.scalar
        def _(act):
            for dst, src in ((w_in[:, 0, :], wu_d), (w_in[:, 1, :], wi_d), (w3[:, :], w3_d),
                             (w2[:, :, :], w2_d.rearrange("k i o -> i k o")),
                             (diag[:, 0:U // P], du_d.rearrange("(t p) -> p t", p=P)),
                             (diag[:, U // P:NT], di_d.rearrange("(t p) -> p t", p=P)),
                             (par[:, 0:2], pu_d.partition_broadcast(P)), (par[:, 2:4], pi_d.partition_broadcast(P)),
                             (gam[:, :], gam_d.partition_broadcast(P)), (bet[:, :], bet_d.partition_broadcast(P)),
                             (b2[:, :], b2_d.partition_broadcast(P)), (b3[:, :], b3_d.partition_broadcast(P))):
                act.dma_start(dst, src, allow_slow_non_contiguous=True).then_inc(consts_in, 16)

            for m in range(NB):
                act.wait_ge(ez_turned, m + 1)
                if m >= 2:
                    act.wait_ge(ez_mult, m - 1)
                nc.scalar.activation(xt2[m % 2][:, :], aux[0][0:D, :], ACT.Copy).then_inc(ez_saved, 1)

            def take_high(n, parity):
                for h in range(HALVES):
                    act.wait_ge(block_turned, n * 2 + (h + 1))
                    if not (isinstance(n, int) and n < 2):
                        act.wait_ge(half_used, n * 2 + (h - 3))
                    nc.scalar.activation(high[:, parity, h * HS:(h + 1) * HS, :], turned[h][:, :, :],
                                         ACT.Copy).then_inc(high_ready, 1)

            def group(g, n0):
                act.wait_ge(t_done, g + 1)
                nc.scalar.activation(xt_sb[:, :], aux[0][0:D, :], ACT.Copy).then_inc(t_saved, 1)
                take_high(n0, 0)
                act.wait_ge(t_turned, g + 1)
                nc.scalar.activation(t_cur[:, :, 0:D], aux[1][:, 0:RD].rearrange("p (a d) -> p a d", d=D),
                                     ACT.Copy).then_inc(t_high, 1)
                for m in range(1, NB):
                    take_high(n0 + m, m % 2)

            group(0, 0)
            with act.Fori(1, NB) as g:
                group(g, g * NB)

            for m in range(NB):
                act.wait_ge(h_rows, m + 1)
                nc.scalar.activation(S[:, m * SUB:(m + 1) * SUB, :], aux[m % 2][:, 0:RD].rearrange("p (a d) -> p a d", d=D),
                                     ACT.Copy).then_inc(h_rows_saved, 1)

            def save_y(r, doubled):
                nc.scalar.activation(y_sb[:, :], acc[0][:, :], ACT.Copy, scale=2.0 if doubled else 1.0).then_inc(y_saved, 1)

            def save_rows(r):
                act.wait_ge(y_rows, r)
                if not (isinstance(r, int) and r < 2):
                    act.wait_ge(rows_taken, r)
                nc.scalar.activation(y_nat, aux[0][:, 0:RD].rearrange("p (a d) -> p a d", d=D),
                                     ACT.Copy).then_inc(y_rows_saved, 1)

            def row(p, m, prev_p):
                first = isinstance(m, int)
                r = m + NB * p
                q = {} if prev_p is None else {j: W_BASE[prev_p] + len(WEIGHTS[prev_p]) * (NB - 1 if first else m - 1) + j
                                               for j in range(len(WEIGHTS[prev_p]))}
                for k in range(NB):
                    n = m * NB + tile_no(p, 0, k)
                    take_high(n, k % 2)
                    if prev_p is None:
                        continue
                    if k == 0:
                        act.wait_ge(half_used, n * 2)
                        save_y(r, prev_p in (2, 3))
                    if k == 1:
                        save_rows(r)
                    for j, (at_turn, at_mult) in enumerate(W_STEP[prev_p]):
                        if k == at_turn:
                            act.wait_ge(feat_turned, q[j] + 1)
                            nc.scalar.activation(xt_sb[:, :], aux[1][0:D, :], ACT.Copy).then_inc(feat_saved, 1)
                        if k == at_mult:
                            act.wait_ge(feat_mult, q[j] + 1)
                            nc.scalar.activation(wy_nat, aux[0][:, RD:2 * RD].rearrange("p (a d) -> p a d", d=D),
                                                 ACT.Copy).then_inc(feat_mult_saved, 1)

            for p in range(PASSES):
                row(p, 0, p - 1 if p else None)
                with act.Fori(1, NB) as m:
                    row(p, m, p)
            act.wait_ge(half_used, tile_no(PASSES, 0, 0) * 2)
            save_y(NB * PASSES, False)
            save_rows(NB * PASSES)

        @block.vector
        def _(dve):
            chain = Chain(dve, dve_step)

            def reduce_last(chain, v, scratch, out):
                chain.step(nc.vector.tensor_reduce(out, v, AX.X, ALU.add))

            def layernorm_all(v, out, square):
                feature_mean_scale(nc.vector, chain, v, out, square, mean[:, :], rstd[:, :], minus_half, reduce_last)

            dve.wait_ge(x_in, 16)
            layernorm_all(X[:, :, :], R[:, :, :], E[:, :, :])
            nc.vector.tensor_scalar(rstd[:, :], rstd[:, :], 1.0, None, ALU.mult).then_inc(var_ready, 1)
            dve.wait_ge(pow_ready, 1)
            whole = [P, NT, D]
            chain.step(nc.vector.tensor_tensor(R[:, :, :], R[:, :, :], rstd[:, :].unsqueeze(2).broadcast_to(whole), ALU.mult))
            chain.step(nc.vector.tensor_scalar(R[:, :, :], R[:, :, :], 0.0, None, ALU.max))
            dve.wait_ge(consts_in, CONST_LOADS)
            nc.vector.tensor_tensor(S[:, :, :], R[:, :, :], diag[:, :].unsqueeze(2).broadcast_to(whole), ALU.mult).then_inc(ez_ready, 1)
            chain.step(nc.vector.tensor_tensor(par[:, 0:1], par[:, 0:1], par[:, 1:2], ALU.mult))
            chain.step(nc.vector.tensor_tensor(par[:, 2:3], par[:, 2:3], par[:, 3:4], ALU.mult))
            for m in range(NB):
                dve.wait_ge(ez_mult, m + 1)
                c = par[:, 0:1] if m * B < U else par[:, 2:3]
                nc.vector.scalar_tensor_tensor(E[:, m * SUB:(m + 1) * SUB, :], aux[1][:, 0:RD].rearrange("p (a d) -> p a d", d=D),
                                               c, R[:, m * SUB:(m + 1) * SUB, :], ALU.mult, ALU.add).then_inc(e_ready, 1)

            def take_low(n, parity):
                for h in range(HALVES):
                    dve.wait_ge(high_ready, n * 2 + (h + 1))
                    part = slice(h * HS, (h + 1) * HS)
                    nc.vector.tensor_tensor(low[:, parity, part, :], turned[h][:, :, :],
                                            high[:, parity, part, :].bitcast(F32), ALU.subtract).then_inc(low_ready, 1)

            def group(g, n0):
                for m in range(NB):
                    dve.wait_ge(raw_in[m], g * 16 + 16)
                    nc.vector.tensor_reduce(deg_part[:, m * SUB:(m + 1) * SUB, bass.ds(g, 1)].rearrange("p a g -> p (a g)")
                                            if not isinstance(g, int) else deg_part[:, m * SUB:(m + 1) * SUB, g],
                                            raw[:, m], AX.X, ALU.add).then_inc(deg_summed, 1)
                take_low(n0, 0)
                dve.wait_ge(t_high, g + 1)
                nc.vector.tensor_tensor(t_cur[:, :, D:2 * D], aux[1][:, 0:RD].rearrange("p (a d) -> p a d", d=D),
                                        t_cur[:, :, 0:D].bitcast(F32), ALU.subtract).then_inc(t_ready, 1)

                def add(m):
                    dve.wait_ge(half_used, (n0 + m) * 2 + 2)
                    if isinstance(g, int) and g == 0:
                        ins = nc.vector.tensor_copy(h_acc[:, m, :], acc[m % 2][:, :])
                    else:
                        ins = nc.vector.tensor_tensor(h_acc[:, m, :], acc[m % 2][:, :], h_acc[:, m, :], ALU.add)
                    ins.then_inc(h_added, 1)
                for m in range(1, NB):
                    take_low(n0 + m, m % 2)
                    add(m - 1)
                add(NB - 1)

            group(0, 0)
            with dve.Fori(1, NB) as g:
                dve.wait_ge(h_added, g * NB)
                group(g, g * NB)

            dve.wait_ge(deg_summed, NB * NB)
            nc.vector.tensor_reduce(dis[:, :], deg_part[:, :, :], AX.X, ALU.add).then_inc(deg_ready, 1)
            dve.wait_ge(h_rows_saved, NB)
            layernorm_all(S[:, :, :], S[:, :, :], E[:, :, :])
            nc.vector.tensor_scalar(rstd[:, :], rstd[:, :], 1.0, None, ALU.mult).then_inc(var_ready, 1)
            dve.wait_ge(pow_ready, 2)
            chain.step(nc.vector.tensor_tensor(S[:, :, :], S[:, :, :], rstd[:, :].unsqueeze(2).broadcast_to(whole), ALU.mult))
            chain.step(nc.vector.tensor_tensor(S[:, :, :], S[:, :, :], gam[:, :].unsqueeze(1).broadcast_to(whole), ALU.mult))
            chain.step(nc.vector.tensor_tensor(S[:, :, :], S[:, :, :], bet[:, :].unsqueeze(1).broadcast_to(whole), ALU.add))
            chain.step(nc.vector.tensor_tensor(S[:, :, :], S[:, :, :], R[:, :, :], ALU.add))
            chain.step(nc.vector.tensor_tensor(X[:, :, :], S[:, :, :], X[:, :, :], ALU.add))
            layernorm_all(X[:, :, :], S[:, :, :], E[:, :, :])
            nc.vector.tensor_scalar(rstd[:, :], rstd[:, :], 1.0, None, ALU.mult).then_inc(var_ready, 1)
            dve.wait_ge(pow_ready, 3)
            chain.step(nc.vector.tensor_tensor(S[:, :, :], S[:, :, :], rstd[:, :].unsqueeze(2).broadcast_to(whole), ALU.mult))
            chain.step(nc.vector.tensor_scalar(S[:, :, :], S[:, :, :], 0.0, None, ALU.max))
            chain.step(nc.vector.tensor_copy(feats_a[:, :, 0:D], S[:, :, :]))
            nc.vector.tensor_tensor(feats_a[:, :, D:2 * D], S[:, :, :], feats_a[:, :, 0:D].bitcast(F32),
                                    ALU.subtract).then_inc(feats_ready, NB)

            with dve.Fori(0, NB * PASSES) as r:
                for k in range(NB):
                    take_low(r * NB + (NB * NB + k), k % 2)

        @block.gpsimd
        def _(pool):
            op = nc.gpsimd
            chain = Chain(pool, pool_step)
            pool.sem_inc(rows_taken, 1)
            chain.step(op.memset(minus_half[:, :], -0.5))
            chain.step(op.memset(ident[:, :], 0.0))
            chain.step(op.memset(fold[:, :], 0.0))
            op.affine_select(out=ident[:, :], in_=ident[:, :], compare_op=ALU.not_equal, fill=1.0, base=0,
                             pattern=[[-1, P]], channel_multiplier=1).then_inc(made, 1)
            op.affine_select(out=fold[:, :], in_=fold[:, :], compare_op=ALU.not_equal, fill=1.0, base=0,
                             pattern=[[-1, D]], channel_multiplier=1).then_inc(made, 1)
            pool.wait_ge(made, 2)
            op.affine_select(out=fold[:, :], in_=fold[:, :], compare_op=ALU.not_equal, fill=1.0, base=-D,
                             pattern=[[-1, D]], channel_multiplier=1).then_inc(made, 1)

            def raise_var(i):
                pool.wait_ge(var_ready, i)
                op.tensor_tensor(rstd[:, :], rstd[:, :], minus_half[:, :], ALU.pow).then_inc(pow_ready, 1)
            raise_var(1)

            pool.wait_ge(deg_ready, 1)
            chain.step(op.tensor_scalar(dis[:, :], dis[:, :], 1.0, None, ALU.add))
            chain.step(op.tensor_scalar(diag[:, :], dis[:, :], 0.0, None, ALU.is_equal))
            chain.step(op.tensor_tensor(dis[:, :], dis[:, :], diag[:, :], ALU.add))
            chain.step(op.tensor_tensor(dis[:, :], dis[:, :], minus_half[:, :], ALU.pow))
            chain.step(op.tensor_scalar(diag[:, :], diag[:, :], -1.0, 1.0, ALU.mult, ALU.add))
            chain.step(op.tensor_tensor(dis[:, :], dis[:, :], diag[:, :], ALU.mult))
            raise_var(2)
            raise_var(3)

            wide = [P, SUB, D]

            def reduce_last(chain, v, scratch, out):
                w = D // 2
                src = v
                while w > 1:
                    chain.step(op.tensor_tensor(scratch[:, :, 0:w], src[:, :, 0:w], src[:, :, w:2 * w], ALU.add))
                    src, w = scratch, w // 2
                chain.step(op.tensor_tensor(out.unsqueeze(2), src[:, :, 0:1], src[:, :, 1:2], ALU.add))

            def layernorm_relu(v, out):
                s, v2 = mean[:, 0:SUB], rstd[:, 0:SUB]
                feature_mean_scale(op, chain, v, centred_row, square_row, s, v2, minus_half, reduce_last)
                chain.step(op.tensor_tensor(v2, v2, minus_half[:, 0:SUB], ALU.pow))
                chain.step(op.tensor_tensor(centred_row, centred_row, v2.unsqueeze(2).broadcast_to(wide), ALU.mult))
                return op.tensor_scalar(out, centred_row, 0.0, None, ALU.max)

            def split(nxt, rows, v):
                chain.step(op.tensor_copy(nxt[:, rows, 0:D], v))
                op.tensor_tensor(nxt[:, rows, D:2 * D], v, nxt[:, rows, 0:D].bitcast(F32), ALU.subtract).then_inc(feats_ready, 1)

            def row(p, m):
                r = m + NB * p
                q = m * len(WEIGHTS[p]) + W_BASE[p]
                rows = bass.ds(m * SUB, SUB)
                pool.wait_ge(y_rows_saved, r + 1)
                pool.wait_ge(rows_taken, r + 1)
                if p == 0:
                    chain.step(op.tensor_tensor(x_row, X[:, rows, :], y_nat, ALU.add))
                    ins = layernorm_relu(x_row, feat_row)
                    chain.step(ins)
                    op.tensor_copy(E[:, rows, :], feat_row).then_inc(feat_rows, 1)
                    split(NEXT[p], rows, feat_row)
                    chain.step(op.tensor_tensor(x_row, x_row, b2[:, :].unsqueeze(1).broadcast_to(wide), ALU.add))
                    pool.wait_ge(feat_mult_saved, q + 1)
                    op.tensor_tensor(X[:, rows, :], x_row, wy_nat, ALU.add).then_inc(rows_taken, 1)
                elif p in (1, 2):
                    if p == 1:
                        pool.sem_inc(pool_held, 1)
                        chain.step(op.tensor_copy(feat_row, y_nat))
                    else:
                        chain.step(op.tensor_tensor(feat_row, y_nat, E[:, rows, :], ALU.subtract))
                    if p == 1:
                        op.tensor_copy(R[:, rows, :], feat_row).then_inc(feat_rows, 1)
                    else:
                        op.tensor_copy(E[:, rows, :], feat_row).then_inc(feat_rows, 1)
                    split(NEXT[p], rows, feat_row)
                    pool.wait_ge(feat_mult_saved, q + 1)
                    op.tensor_tensor(X[:, rows, :], X[:, rows, :], wy_nat, ALU.add).then_inc(rows_taken, 1)
                elif p == 3:
                    op.tensor_tensor(feat_row, y_nat, R[:, rows, :], ALU.subtract).then_inc(feat_rows, 1)
                    pool.wait_ge(feat_mult_saved, q + 1)
                    chain.step(op.tensor_tensor(x_row, X[:, rows, :], wy_nat, ALU.add))
                    chain.step(op.tensor_copy(X[:, rows, :], x_row))
                    layernorm_relu(x_row, feat_row).then_inc(feat_rows, 1)
                    pool.wait_ge(feat_mult_saved, q + 2)
                    op.tensor_tensor(gs_row, wy_nat, b3[:, :].unsqueeze(1).broadcast_to(wide), ALU.add).then_inc(rows_taken, 1)
                    pool.wait_ge(rows_taken, r + 2)
                    chain.step(op.tensor_tensor(gs_row, gs_row, dis[:, rows].unsqueeze(2).broadcast_to(wide), ALU.mult))
                    chain.step(op.tensor_copy(E[:, rows, :], gs_row))
                    split(NEXT[p], rows, gs_row)
                else:
                    op.tensor_tensor(gs_row, y_nat, E[:, rows, :], ALU.add).then_inc(rows_taken, 1)
                    pool.wait_ge(rows_taken, r + 2)
                    chain.step(op.tensor_tensor(gs_row, gs_row, dis[:, rows].unsqueeze(2).broadcast_to(wide), ALU.mult))
                    chain.step(op.tensor_scalar(gs_row, gs_row, 0.0, None, ALU.max))
                    if not isinstance(m, int):
                        pool.wait_ge(out_stored, m * 16)
                    op.tensor_tensor(out_rows[:, 0], gs_row, X[:, rows, :], ALU.add).then_inc(out_ready, 1)
                    pool.wait_ge(out_ready, m + 1)
                    pool.dma_start(out_v[:, bass.ds(m, 1), :, :].rearrange("p m a d -> p (m a) d"), out_rows[:, 0]).then_inc(out_stored, 16)

            for p in range(PASSES):
                if p == PASSES - 1:
                    chain.restart()
                    row(p, 0)
                with pool.Fori(1 if p == PASSES - 1 else 0, NB) as m:
                    chain.restart()
                    row(p, m)
            pool.wait_ge(out_stored, 16 * NB)


_INS = ['x', 'adj', 'L0_gnn_W_u', 'L0_gnn_diag_u', 'L0_gnn_par_u', 'L0_gnn_W_i', 'L0_gnn_diag_i', 'L0_gnn_par_i',
        'L0_gnn_ln_gamma', 'L0_gnn_ln_beta', 'L2_gnn_weights', 'L2_gnn_bias', 'L3_gnn_W', 'L3_gnn_b']


def kernel(**inputs):
    import numpy as _np
    import concourse.bacc as _bacc
    from concourse import mybir as _mybir
    from concourse.bass_utils import run_bass_kernel_spmd as _run

    nc = _bacc.Bacc("TRN2", target_bir_lowering=False, num_devices=1)
    arrays, args = {}, []
    for name in _INS:
        a = _np.ascontiguousarray(inputs[name])
        arrays[f"in_{name}_dram"] = a
        args.append(nc.dram_tensor(f"in_{name}_dram", a.shape, _mybir.dt.from_np(a.dtype), kind="ExternalInput").ap())
    out = nc.dram_tensor("out_dram", (N, D), _mybir.dt.float32, kind="ExternalOutput").ap()
    gnn_stack(nc, *args, out)
    r = _run(nc, [arrays], core_ids=[0])
    return r.results[0]["out_dram"]
```

```python
import concourse.bass as bass
from concourse import mybir
from contextlib import ExitStack
import numpy as np

F32 = mybir.dt.float32
F32R = mybir.dt.float32r
ALU = mybir.AluOpType
ACT = mybir.ActivationFunctionType
AX = mybir.AxisListType

P = 128
N = 5120
D = 64
U = 2048
B = 512
SUB = B // P
NB = N // B
NT = N // P
HALVES = 2
HS = SUB // HALVES
PASSES = 5
SLOTS = 4
LAG = 2
SUM_LAG = 1
OWN_BANKS = 3
EPS = 1e-5
RD = SUB * D



class Chain:

    def __init__(self, eng, sem):
        self.eng, self.sem, self.n = eng, sem, 0

    def step(self, ins):
        ins.then_inc(self.sem, 1)
        self.n += 1
        self.eng.wait_ge(self.sem, self.n)


WEIGH = [(5,), (3,), (3,), (3, 7), ()]
MAKE = [(4,), (), (2,), (2, 7, 9), ()]
SPLIT = [5, 3, 3, 10, None]


class Plan:

    def __init__(self):
        self.tiles = []
        self.step_tile = []
        self.rows = []
        self.ended = {}
        self.row_no = {}
        self.end_step = {}
        self.first_own, self.last_own, self.first_dual, self.last_dual = {}, {}, {}, {}
        self.dual_rows = []
        self.has_part = set()
        ready = {(0, m): 0 for m in range(NB)}
        turns = set()
        covered = {(0, m): set() for m in range(NB)}
        for p in range(PASSES):
            order = list(range(NB)) if p % 2 == 0 else list(range(NB))[::-1]
            cols = {m: [k for k in order if k not in covered[p, m]] for m in order}
            late = order[0] if p else None
            seq = []
            head = order[:OWN_BANKS] if p else []
            seq += [(m, k) for m in head for k in cols[m] if k != late]
            seq += [(m, k) for m in head for k in cols[m] if k == late]
            seq += [(m, k) for m in order if m not in head for k in cols[m]]
            left = {m: len(cols[m]) for m in order}
            for m in order:
                covered[p + 1, m] = set()
            for m, k in seq:
                while ready[p, k] > len(self.step_tile) or \
                        left[m] == 1 and turns & {len(self.step_tile) + d for d in WEIGH[p]}:
                    self.step_tile.append(None)
                step, n = len(self.step_tile), len(self.tiles)
                dual = p + 1 < PASSES and ready.get((p + 1, k), 1 << 30) <= step + LAG
                self.step_tile.append(n)
                self.tiles.append((p, m, k, dual))
                self.first_own.setdefault((p, m), n)
                self.last_own[p, m] = n
                if dual:
                    covered[p + 1, m].add(k)
                    if (p + 1, m) not in self.first_dual:
                        self.first_dual[p + 1, m] = n
                        self.dual_rows.append((p + 1, m))
                    self.last_dual[p + 1, m] = n
                left[m] -= 1
                if left[m] == 0:
                    turns |= {step + d for d in WEIGH[p]}
                    self.row_no[p, m] = len(self.rows)
                    self.end_step[p, m] = step
                    self.ended.setdefault(step, []).append(len(self.rows))
                    self.rows.append((p, m))
                    if SPLIT[p] is not None:
                        ready[p + 1, m] = step + SPLIT[p]
        self.tile_step = {n: s for s, n in enumerate(self.step_tile) if n is not None}
        self.steps = len(self.step_tile) + 6
        self.step_tile += [None] * 6
        turns = sorted((self.end_step[p, m] + d, self.row_no[p, m], j)
                       for (p, m) in self.rows for j, d in enumerate(WEIGH[p]))
        self.weigh_no = {(r, j): q for q, (_, r, j) in enumerate(turns)}
        self.own_no, self.dual_no, count = {}, {}, 0
        for s, n in enumerate(self.step_tile):
            if n is not None:
                count += 1
                self.own_no[n] = count
            n = self.step_tile[s - LAG] if s >= LAG else None
            if n is not None and self.tiles[n][3]:
                count += 1
                self.dual_no[n] = count
        events = sorted((self.end_step[p, m] + d, -d, self.row_no[p, m], j)
                        for (p, m) in self.rows for j, d in enumerate(MAKE[p]))
        self.made_no = {(r, j): i + 1 for i, (_, _, r, j) in enumerate(events)}
        self.part_saved_in = {}
        for i, row in enumerate(self.dual_rows):
            p, m = row
            s = max(self.tile_step[self.last_dual[row]] + LAG, self.end_step[p - 1, m]) + 2
            self.part_saved_in.setdefault(s, []).append(i)

    def used_no(self, n):
        return self.dual_no.get(n, self.own_no[n])

    def rows_at(self, step, delay, *passes):
        return [r for r in self.ended.get(step - delay, []) if self.rows[r][0] in passes]

    def turns_at(self, step, delay=0):
        return [(r, j) for r, (p, m) in enumerate(self.rows) for j, d in enumerate(WEIGH[p])
                if self.end_step[p, m] + d == step - delay]


def gnn_stack(nc, x_d, adj_d, wu_d, du_d, pu_d, wi_d, di_d, pi_d, gam_d, bet_d, w2_d, b2_d, w3_d, b3_d, out_d):
    plan = Plan()
    ctx = ExitStack()
    with ctx:
        def sb(name, shape, dt=F32, stack=ctx):
            return stack.enter_context(nc.sbuf_tensor(name, shape, dt))

        def sem(name):
            return ctx.enter_context(nc.semaphore(name))

        adj_t = nc.dram_tensor("adj_t", (NB, NB, P, SUB, B), F32, kind="Internal").ap()

        whole = [sb(f"whole{s}", [P, SUB, B]) for s in range(2)]
        high = [sb(f"high{s}", [P, SUB, B], F32R) for s in range(2)]
        low = [sb(f"low{s}", [P, SUB, B], F32R) for s in range(2)]
        X = sb("X", [P, NT, D])
        E = sb("E", [P, NT, D])
        R = sb("R", [P, NT, D])
        t_cur = sb("t_cur", [P, SUB, 2 * D], F32R)
        deg_part = sb("deg_part", [P, NT, NB])
        dis = sb("dis", [P, NT])
        diag = sb("diag", [P, NT])
        par = sb("par", [P, 4])
        total = sb("total", [P, NT])
        rstd = sb("rstd", [P, NT])
        minus_half = sb("minus_half", [P, NT])
        gam = sb("gam", [P, D])
        bet = sb("bet", [P, D])
        b2 = sb("b2", [P, D])
        b3 = sb("b3", [P, D])
        w_in = sb("w_in", [D, 2, D])
        w2 = sb("w2", [D, 4, D])
        w3 = sb("w3", [D, D])
        ident = sb("ident", [P, P])
        fold = sb("fold", [P, D])
        with ExitStack() as early:
            raw = sb("raw", [P, NB, SUB, B], F32, early)
            h_acc = sb("h_acc", [P, NB, B], F32, early)
            S = sb("S", [P, NT, D], F32, early)
            ego_t = [sb(f"ego_t{i}", [D, B], F32, early) for i in range(2)]
            sq_early = [sb(f"sq_early{i}", [P, SUB, D], F32, early) for i in range(2)]
        whole += [sb(f"whole{s}", [P, SUB, B]) for s in range(2, SLOTS)]
        high += [sb(f"high{s}", [P, SUB, B], F32R) for s in range(2, SLOTS)]
        low += [sb(f"low{s}", [P, SUB, B], F32R) for s in range(2, SLOTS)]
        part = sb("part", [P, NB, B])
        y_sb = [sb(f"y_sb{i}", [P, B]) for i in range(2)]
        feat_t = [sb(f"feat_t{i}", [D, B]) for i in range(2)]
        cen = [sb(f"cen{i}", [P, SUB, D]) for i in range(2)]
        sq = [sb(f"sq{i}", [P, SUB, D]) for i in range(2)]
        feats = [None, sb("feats1", [P, NT, 2 * D], F32R)]
        feats[0] = sb("feats0", [P, NT, 2 * D], F32R)
        out_rows = sq

        turned = [ctx.enter_context(nc.psum_tensor(f"turned{h}", [P, HS, B], F32)) for h in range(HALVES)]
        acc = [ctx.enter_context(nc.psum_tensor(f"acc{i}", [P, B], F32)) for i in range(2)]
        aux = [ctx.enter_context(nc.psum_tensor(f"aux{i}", [P, B], F32)) for i in range(2)]
        own_bank = [acc[0][:, :], acc[1][:, :], turned[0][:, 0, :]]
        dual_bank = [turned[1][:, 0, :], turned[1][:, 1, :]]
        weighed = turned[0][:, 1, 0:RD].rearrange("p (a d) -> p a d", d=D)
        aux_rows = [a[:, 0:RD].rearrange("p (a d) -> p a d", d=D) for a in aux]

        raw_in = [sem(f"raw_in{s}") for s in range(NB)]
        whole_in = [sem(f"whole_in{s}") for s in range(SLOTS)]
        stored = [sem(f"stored{s}") for s in range(2)]
        weights_in = sem("weights_in")
        vectors_in = sem("vectors_in")
        x_in = sem("x_in")
        made = sem("made")
        half_turned = sem("half_turned")
        half_copied = sem("half_copied")
        high_ready = sem("high_ready")
        low_ready = sem("low_ready")
        used = sem("used")
        deg_summed = sem("deg_summed")
        h_added = sem("h_added")
        t_done = sem("t_done")
        t_high = sem("t_high")
        t_ready = sem("t_ready")
        centred = sem("centred")
        squared = sem("squared")
        var_ready = sem("var_ready")
        pow_ready = sem("pow_ready")
        ego_ready = sem("ego_ready")
        ego_turned = sem("ego_turned")
        ego_copied = sem("ego_copied")
        ego_mult = sem("ego_mult")
        e_ready = sem("e_ready")
        h_rows = sem("h_rows")
        multiplied = sem("multiplied")
        part_saved = sem("part_saved")
        y_saved = sem("y_saved")
        y_rows = sem("y_rows")
        y_copied = sem("y_copied")
        y_read = sem("y_read")
        rows_ready = sem("rows_ready")
        upper_ready = sem("upper_ready")
        feats_ready = sem("feats_ready")
        feat_turned = sem("feat_turned")
        feat_copied = sem("feat_copied")
        feat_mult = sem("feat_mult")
        mult_read = sem("mult_read")
        deg_ready = sem("deg_ready")
        dis_ready = sem("dis_ready")
        out_ready = sem("out_ready")
        out_stored = [sem(f"out_stored{i}") for i in range(2)]
        act_step = sem("act_step")
        dve_step = sem("dve_step")
        pool_step = sem("pool_step")

        adj_v = adj_d.rearrange("(m a p) (g k) -> p m a g k", a=SUB, p=P, k=B)
        x_v = x_d.rearrange("(t p) d -> p t d", p=P)
        out_v = out_d.rearrange("(m a p) d -> p m a d", a=SUB, p=P)
        adj_t_v = adj_t.rearrange("m k p a n -> p m k (a n)")
        WEIGHTS = [(w2[:, 0, :],), (w2[:, 1, :],), (w2[:, 2, :],), (w2[:, 3, :], w3[:, :]), ()]
        SOURCE = [(E,), (R,), (E,), (R, R), ()]
        MADE = [E, R, E, E]
        LN_START = [("start", m) for m in range(NB)]
        LN_H = [x for i in range(NB + 2) for x in ((("h", i),) if i < NB else ()) + ((("x", i - 2),) if i >= 2 else ())]
        LN_PASS = [(p, m) for p, m in plan.rows if p in (0, 3)]
        LN_NO = {x: i for i, x in enumerate(LN_START + LN_H + LN_PASS)}

        def features_made(r, j):
            return NB + plan.made_no[r, j]

        def of(m):
            return slice(m * SUB, (m + 1) * SUB)

        row_shape = [P, SUB, D]

        def over_features(v):
            return v.unsqueeze(2).broadcast_to(row_shape)

        def over_nodes(v):
            return v[:, :].unsqueeze(1).broadcast_to(row_shape)

        N_STEPS = plan.steps
        DUAL_NO = {row: i for i, row in enumerate(plan.dual_rows)}
        TOTAL_TILES = NB * NB

        block = ctx.enter_context(nc.Block())

        @block.sync
        def _(sp):
            sp.dma_start(X[:, :, :], x_v).then_inc(x_in, 16)
            for m in range(NB):
                sp.dma_start(raw[:, m], adj_v[:, m, :, 0, :]).then_inc(raw_in[m], 16)

            def store(g, m):
                sp.wait_ge(half_copied, g * (NB * 2) + (2 * m + 2))
                src = whole[m % 2][:, :, :].rearrange("p a n -> p (a n)")
                dst = adj_t_v[:, m, g] if isinstance(g, int) else \
                    adj_t_v[:, m, bass.ds(g, 1), :].rearrange("p g n -> p (g n)")
                sp.dma_start(dst, src).then_inc(stored[m % 2], 16)

            def load_next(g, m):
                sp.wait_ge(half_turned, g * (NB * 2) + (2 * m + 2))
                src = adj_v[:, m, :, g + 1, :] if isinstance(g, int) else \
                    adj_v[:, m, :, bass.ds(g + 1, 1), :].rearrange("p a g k -> p a (g k)")
                sp.dma_start(raw[:, m], src).then_inc(raw_in[m], 16)

            def group(g):
                for m in range(NB):
                    load_next(g, m)
                    store(g, m)

            group(0)
            with sp.Fori(1, NB - 1) as g:
                group(g)
            for m in range(NB):
                store(NB - 1, m)
            for s in range(2):
                sp.wait_ge(stored[s], 16 * TOTAL_TILES // 2)
            for n, (p, m, k, dual) in enumerate(plan.tiles):
                if n >= SLOTS:
                    sp.wait_ge(low_ready, TOTAL_TILES + n - SLOTS + 1)
                elif n < 2:
                    sp.wait_ge(low_ready, TOTAL_TILES)
                sp.dma_start(whole[n % SLOTS][:, :, :].rearrange("p a n -> p (a n)"), adj_t_v[:, m, k]) \
                    .then_inc(whole_in[n % SLOTS], 16)

        @block.tensor
        def _(pe):
            def multiply(v, slot, bank, start, stop):
                for i in range(SUB):
                    for piece in (high, low):
                        last = nc.tensor.matmul(bank, v[:, i, :], piece[slot][:, i, :],
                                                start=start and i == 0 and piece is high,
                                                stop=stop and i == SUB - 1 and piece is low)
                return last

            pe.wait_ge(made, 3)
            for m in range(NB + 1):
                if m < NB:
                    pe.wait_ge(ego_ready, m + 1)
                    if m >= 1:
                        pe.wait_ge(ego_copied, m)
                    for a in range(SUB):
                        last = nc.tensor.transpose(aux[0][0:D, a * P:(a + 1) * P], S[:, m * SUB + a, :], ident[:, :])
                    last.then_inc(ego_turned, 1)
                if m >= 1:
                    r = m - 1
                    if r == 0:
                        pe.wait_ge(weights_in, 16 * 4)
                    pe.wait_ge(ego_copied, r + 1)
                    if r >= 1:
                        pe.wait_ge(e_ready, r)
                    for a in range(SUB):
                        last = nc.tensor.matmul(aux[1][:, a * D:(a + 1) * D], ego_t[r % 2][:, a * P:(a + 1) * P],
                                                w_in[:, 0 if r * B < U else 1, :], start=True, stop=True)
                    last.then_inc(ego_mult, 1)

            def turn(g, m):
                pe.wait_ge(deg_summed, g * NB + (m + 1))
                for h in range(HALVES):
                    if not (isinstance(g, int) and g * NB + m == 0):
                        pe.wait_ge(half_copied, g * (NB * 2) + (2 * m + h - 1))
                    for b in range(HS):
                        for a in range(SUB):
                            last = nc.tensor.transpose(turned[h][:, b, a * P:(a + 1) * P],
                                                       raw[:, m % NB, a, (h * HS + b) * P:(h * HS + b + 1) * P],
                                                       ident[:, :])
                    last.then_inc(half_turned, 1)

            def products_for_t(g, m):
                pe.wait_ge(raw_in[m], g * 16 + 16)
                for a in range(SUB):
                    for b in range(SUB):
                        last = nc.tensor.matmul(aux[0][:, b * D:(b + 1) * D], raw[:, m, a, b * P:(b + 1) * P],
                                                E[:, m * SUB + a, :], start=(m == 0 and a == 0 and b == 0),
                                                stop=(m == NB - 1 and a == SUB - 1), skip_group_check=True)
                if m == NB - 1:
                    last.then_inc(t_done, 1)

            def group(g, followed=True):
                first = isinstance(g, int) and g == 0
                for m in range(NB):
                    if m + 1 < NB or followed:
                        turn(g, m + 1)
                    if m == 0:
                        pe.wait_ge(t_ready, g + 1)
                    pe.wait_ge(low_ready, g * NB + (m + 1))
                    if not (first and m < 2):
                        pe.wait_ge(h_added, g * NB + (m - 1))
                    multiply(t_cur, m % 2, acc[m % 2][:, :], True, True).then_inc(used, 1)
                    if followed:
                        products_for_t(g + 1, m)

            pe.wait_ge(ego_copied, NB)
            for m in range(NB):
                pe.wait_ge(e_ready, m + 1)
                products_for_t(0, m)
            turn(0, 0)
            group(0)
            with pe.Fori(1, NB - 1) as g:
                group(g)
            group(NB - 1, followed=False)

            pe.wait_ge(h_added, TOTAL_TILES)
            for m in range(NB):
                if m >= 2:
                    pe.wait_ge(centred, LN_NO["h", m - 2] + 1)
                for a in range(SUB):
                    last = nc.tensor.matmul(aux[m % 2][:, a * D:(a + 1) * D], h_acc[:, m, a * P:(a + 1) * P], fold[:, :],
                                            start=True, stop=True)
                last.then_inc(h_rows, 1)
            pe.wait_ge(centred, LN_NO["h", NB - 1] + 1)

            def aux_read(pe, r):
                p = plan.rows[r][0]
                if p == 0:
                    pe.wait_ge(y_read, r + 1)
                elif p == 1:
                    pe.wait_ge(feats_ready, NB + r + 1)
                elif p in (2, 3):
                    pe.wait_ge(rows_ready, features_made(r, 0))
                else:
                    pe.wait_ge(y_read, r - 3 * NB + 1)

            for s in range(N_STEPS):
                n = plan.step_tile[s]
                if n is not None:
                    p, m, k, dual = plan.tiles[n]
                    pe.wait_ge(low_ready, TOTAL_TILES + n + 1)
                    pe.wait_ge(feats_ready, k + 1 if p == 0 else NB + plan.row_no[p - 1, k] + 1)
                    first, last_one = plan.first_own[p, m] == n, plan.last_own[p, m] == n
                    number = NB * p + (m if p % 2 == 0 else NB - 1 - m)
                    if first and number >= OWN_BANKS:
                        pe.wait_ge(y_saved, number - OWN_BANKS + 1)
                    multiply(feats[p % 2][:, of(k)], n % SLOTS, own_bank[number % OWN_BANKS], first, last_one) \
                        .then_inc(multiplied, 1)
                for r in plan.rows_at(s, 1, *range(PASSES)):
                    pe.wait_ge(y_saved, r + 1)
                    if r >= 1:
                        aux_read(pe, r - 1)
                    for a in range(SUB):
                        last = nc.tensor.matmul(aux[0][:, a * D:(a + 1) * D], y_sb[r % 2][:, a * P:(a + 1) * P],
                                                fold[:, :], start=True, stop=True)
                    last.then_inc(y_rows, 1)
                for r, j in plan.turns_at(s):
                    q, (p, m) = plan.weigh_no[r, j], plan.rows[r]
                    if p == 1:
                        pe.wait_ge(y_copied, r - NB + 1)
                    else:
                        pe.wait_ge(rows_ready, features_made(r, j))
                    if q >= 1:
                        pe.wait_ge(feat_copied, q)
                    for a in range(SUB):
                        last = nc.tensor.transpose(aux[1][0:D, a * P:(a + 1) * P], SOURCE[p][j][:, m * SUB + a, :], ident[:, :])
                    last.then_inc(feat_turned, 1)
                for r, j in plan.turns_at(s, 1):
                    q, (p, m) = plan.weigh_no[r, j], plan.rows[r]
                    pe.wait_ge(feat_copied, q + 1)
                    if q >= 1:
                        pe.wait_ge(mult_read, q)
                    for a in range(SUB):
                        last = nc.tensor.matmul(weighed[:, a, :], feat_t[q % 2][:, a * P:(a + 1) * P], WEIGHTS[p][j],
                                                start=True, stop=True)
                    last.then_inc(feat_mult, 1)
                n = plan.step_tile[s - LAG] if s >= LAG else None
                if n is not None and plan.tiles[n][3]:
                    p, m, k, _ = plan.tiles[n]
                    row = (p + 1, m)
                    i = DUAL_NO[row]
                    pe.wait_ge(feats_ready, NB + plan.row_no[p, k] + 1)
                    first, last_one = plan.first_dual[row] == n, plan.last_dual[row] == n
                    if first and i >= 2:
                        pe.wait_ge(part_saved, i - 1)
                    multiply(feats[(p + 1) % 2][:, of(k)], n % SLOTS, dual_bank[i % 2], first, last_one) \
                        .then_inc(multiplied, 1)

        @block.scalar
        def _(act):
            chain = Chain(act, act_step)
            for dst, src in ((w_in[:, 0, :], wu_d), (w_in[:, 1, :], wi_d), (w3[:, :], w3_d),
                             (w2[:, :, :], w2_d.rearrange("k i o -> i k o"))):
                act.dma_start(dst, src).then_inc(weights_in, 16)
            for dst, src in ((diag[:, 0:U // P], du_d.rearrange("(t p) -> p t", p=P)),
                             (diag[:, U // P:NT], di_d.rearrange("(t p) -> p t", p=P)),
                             (par[:, 0:2], pu_d.partition_broadcast(P)), (par[:, 2:4], pi_d.partition_broadcast(P)),
                             (gam[:, :], gam_d.partition_broadcast(P)), (bet[:, :], bet_d.partition_broadcast(P)),
                             (b2[:, :], b2_d.partition_broadcast(P)), (b3[:, :], b3_d.partition_broadcast(P))):
                act.dma_start(dst, src, allow_slow_non_contiguous=True).then_inc(vectors_in, 16)

            def square(row, v, out):
                act.wait_ge(centred, LN_NO[row] + 1)
                nc.scalar.activation(out, v, ACT.Square).then_inc(squared, 1)

            def copy_ego(m):
                act.wait_ge(ego_turned, m + 1)
                if m >= 2:
                    act.wait_ge(ego_mult, m - 1)
                nc.scalar.activation(ego_t[m % 2][:, :], aux[0][0:D, :], ACT.Copy).then_inc(ego_copied, 1)

            for m in range(NB + 2):
                if m < NB:
                    square(("start", m), R[:, of(m), :], sq_early[m % 2][:, :, :])
                if m >= 2:
                    copy_ego(m - 2)

            def copy_turned(g, m):
                for h in range(HALVES):
                    act.wait_ge(half_turned, g * (NB * 2) + (2 * m + h + 1))
                    if h == 0 and not (isinstance(g, int) and g * NB + m < 2):
                        act.wait_ge(stored[m % 2], g * (16 * NB // 2) + 16 * (m // 2))
                        act.wait_ge(low_ready, g * NB + (m - 1))
                    nc.scalar.activation(whole[m % 2][:, h * HS:(h + 1) * HS, :], turned[h][:, :, :],
                                         ACT.Copy).then_inc(half_copied, 1)

            def take_high(g, m):
                act.wait_ge(half_copied, g * (NB * 2) + (2 * m + 2))
                if not (isinstance(g, int) and g * NB + m < 2):
                    act.wait_ge(used, g * NB + (m - 1))
                nc.scalar.activation(high[m % 2][:, :, :], whole[m % 2][:, :, :], ACT.Copy).then_inc(high_ready, 1)

            def take_t_high(g):
                act.wait_ge(t_done, g + 1)
                if not isinstance(g, int) or g > 0:
                    act.wait_ge(used, g * NB)
                nc.scalar.activation(t_cur[:, :, 0:D], aux_rows[0], ACT.Copy).then_inc(t_high, 1)

            def group(g, followed=True):
                for m in range(1, NB + 1 if followed else NB):
                    copy_turned(g, m)
                    take_high(g, m)
                if followed:
                    take_t_high(g + 1)

            copy_turned(0, 0)
            take_high(0, 0)
            take_t_high(0)
            group(0)
            with act.Fori(1, NB - 1) as g:
                group(g)
            group(NB - 1, followed=False)

            for i in range(NB + 5):
                if i < NB:
                    square(("h", i), E[:, of(i), :], sq[i % 2][:, :, :])
                if 0 <= i - 2 < NB:
                    square(("x", i - 2), E[:, of(i - 2), :], cen[i % 2][:, :, :])
                if 0 <= i - 4 < NB:
                    act.wait_ge(rows_ready, i - 4 + 1)
                    nc.scalar.activation(feats[0][:, of(i - 4), 0:D], R[:, of(i - 4), :], ACT.Copy).then_inc(upper_ready, 1)

            for s in range(N_STEPS):
                n = plan.step_tile[s]
                if n is not None:
                    slot = n % SLOTS
                    act.wait_ge(whole_in[slot], 16 * (n // SLOTS + 1))
                    if n >= SLOTS:
                        act.wait_ge(multiplied, plan.used_no(n - SLOTS))
                    nc.scalar.activation(high[slot][:, :, :], whole[slot][:, :, :], ACT.Copy).then_inc(high_ready, 1)
                for i in plan.part_saved_in.get(s, []):
                    p, m = plan.dual_rows[i]
                    act.wait_ge(multiplied, plan.dual_no[plan.last_dual[p, m]])
                    act.wait_ge(y_saved, plan.row_no[p - 1, m] + 1)
                    nc.scalar.activation(part[:, m, :], dual_bank[i % 2], ACT.Copy).then_inc(part_saved, 1)
                for r in plan.rows_at(s, 3, 1):
                    p, m = plan.rows[r]
                    act.wait_ge(y_rows, r + 1)
                    nc.scalar.activation(R[:, of(m), :], aux_rows[0], ACT.Copy).then_inc(y_copied, 1)
                    nc.scalar.activation(feats[0][:, of(m), 0:D], aux_rows[0], ACT.Copy).then_inc(upper_ready, 1)
                for r in plan.rows_at(s, 3, 0) + plan.rows_at(s, 6, 3):
                    square(plan.rows[r], cen[r % 2][:, :, :], sq[r % 2][:, :, :])
                for r in plan.rows_at(s, 5, 0) + plan.rows_at(s, 3, 2) + plan.rows_at(s, 10, 3):
                    p, m = plan.rows[r]
                    act.wait_ge(rows_ready, features_made(r, len(MAKE[p]) - 1))
                    nc.scalar.activation(feats[(p + 1) % 2][:, of(m), 0:D], MADE[p][:, of(m), :], ACT.Copy).then_inc(upper_ready, 1)
                for r, j in plan.turns_at(s, 2):
                    q = plan.weigh_no[r, j]
                    act.wait_ge(feat_turned, q + 1)
                    if q >= 2:
                        act.wait_ge(feat_mult, q - 1)
                    nc.scalar.activation(feat_t[q % 2][:, :], aux[1][0:D, :], ACT.Copy).then_inc(feat_copied, 1)
                for r in plan.rows_at(s, 4, 4):
                    p, m = plan.rows[r]
                    i = r - 4 * NB
                    act.wait_ge(out_ready, i + 1)
                    act.dma_start(out_v[:, m], out_rows[i % 2][:, :, :]).then_inc(out_stored[i % 2], 16)
            for i in range(2):
                act.wait_ge(out_stored[i], 16 * NB // 2)

        @block.vector
        def _(dve):
            chain = Chain(dve, dve_step)
            stt = nc.vector.scalar_tensor_tensor

            def centre(row, v, m, out):
                chain.step(nc.vector.tensor_reduce(total[:, of(m)], v, AX.X, ALU.add))
                stt(out, over_features(total[:, of(m)]), -1.0 / D, v, ALU.mult, ALU.add).then_inc(centred, 1)

            def variance(row, squares, m):
                dve.wait_ge(squared, LN_NO[row] + 1)
                chain.step(nc.vector.tensor_reduce(rstd[:, of(m)], squares, AX.X, ALU.add))
                nc.vector.tensor_scalar(rstd[:, of(m)], rstd[:, of(m)], 1.0 / D, EPS, ALU.mult, ALU.add).then_inc(var_ready, 1)

            def relu_norm(row, c, m, out):
                dve.wait_ge(pow_ready, LN_NO[row] + 1)
                return stt(out, c, 0.0, over_features(rstd[:, of(m)]), ALU.max, ALU.mult)

            dve.wait_ge(x_in, 16)
            for i in range(NB + 4):
                if i < NB:
                    centre(("start", i), X[:, of(i), :], i, R[:, of(i), :])
                if 0 <= i - 1 < NB:
                    variance(("start", i - 1), sq_early[(i - 1) % 2][:, :, :], i - 1)
                if 0 <= i - 2 < NB:
                    m = i - 2
                    chain.step(relu_norm(("start", m), R[:, of(m), :], m, R[:, of(m), :]))
                    if m == 0:
                        dve.wait_ge(vectors_in, 16 * 8)
                        chain.step(nc.vector.tensor_tensor(par[:, 0:1], par[:, 0:1], par[:, 1:2], ALU.mult))
                        chain.step(nc.vector.tensor_tensor(par[:, 2:3], par[:, 2:3], par[:, 3:4], ALU.mult))
                    nc.vector.tensor_tensor(S[:, of(m), :], R[:, of(m), :], over_features(diag[:, of(m)]),
                                            ALU.mult).then_inc(ego_ready, 1)
                if 0 <= i - 4 < NB:
                    m = i - 4
                    dve.wait_ge(ego_mult, m + 1)
                    stt(E[:, of(m), :], aux_rows[1], par[:, 0:1] if m * B < U else par[:, 2:3], R[:, of(m), :],
                        ALU.mult, ALU.add).then_inc(e_ready, 1)

            def sum_rows(g, m):
                dve.wait_ge(raw_in[m], g * 16 + 16)
                out = deg_part[:, of(m), g] if isinstance(g, int) else \
                    deg_part[:, of(m), bass.ds(g, 1)].rearrange("p a g -> p (a g)")
                nc.vector.tensor_reduce(out, raw[:, m], AX.X, ALU.add).then_inc(deg_summed, 1)

            def take_t_rest(g):
                dve.wait_ge(t_high, g + 1)
                nc.vector.tensor_tensor(t_cur[:, :, D:2 * D], aux_rows[0], t_cur[:, :, 0:D].bitcast(F32),
                                        ALU.subtract).then_inc(t_ready, 1)

            def take_low(g, m):
                dve.wait_ge(high_ready, g * NB + (m + 1))
                nc.vector.tensor_tensor(low[m % 2][:, :, :], whole[m % 2][:, :, :],
                                        high[m % 2][:, :, :].bitcast(F32), ALU.subtract).then_inc(low_ready, 1)

            def add_h(g, m):
                dve.wait_ge(used, g * NB + (m + 1))
                if isinstance(g, int) and g == 0:
                    ins = nc.vector.tensor_copy(h_acc[:, m, :], acc[m % 2][:, :])
                else:
                    ins = nc.vector.tensor_tensor(h_acc[:, m, :], acc[m % 2][:, :], h_acc[:, m, :], ALU.add)
                ins.then_inc(h_added, 1)

            def group(g, followed=True):
                for m in range(NB):
                    if m + 1 < NB or followed:
                        take_low(g, m + 1)
                    if m == 0 and not (isinstance(g, int) and g == 0):
                        dve.wait_ge(h_added, g * NB)
                    if m == NB - 1 and followed:
                        take_t_rest(g + 1)
                    add_h(g, m)
                    if followed and m >= SUM_LAG:
                        sum_rows(g + 1, m - SUM_LAG)
                if followed:
                    for m in range(NB - SUM_LAG, NB):
                        sum_rows(g + 1, m)

            for m in range(NB):
                sum_rows(0, m)
            take_low(0, 0)
            take_t_rest(0)
            group(0)
            with dve.Fori(1, NB - 1) as g:
                group(g)
            group(NB - 1, followed=False)

            dve.wait_ge(deg_summed, TOTAL_TILES)
            nc.vector.tensor_reduce(dis[:, :], deg_part[:, :, :], AX.X, ALU.add).then_inc(deg_ready, 1)
            for i in range(NB + 5):
                if i < NB:
                    dve.wait_ge(h_rows, i + 1)
                    chain.step(nc.vector.tensor_reduce(total[:, of(i)], aux_rows[i % 2], AX.X, ALU.add))
                    stt(E[:, of(i), :], over_features(total[:, of(i)]), -1.0 / D, aux_rows[i % 2],
                        ALU.mult, ALU.add).then_inc(centred, 1)
                if 0 <= i - 1 < NB:
                    variance(("h", i - 1), sq[(i - 1) % 2][:, :, :], i - 1)
                if 0 <= i - 2 < NB:
                    m = i - 2
                    dve.wait_ge(pow_ready, LN_NO["h", m] + 1)
                    e, x = E[:, of(m), :], X[:, of(m), :]
                    chain.step(nc.vector.tensor_tensor(e, e, over_features(rstd[:, of(m)]), ALU.mult))
                    chain.step(nc.vector.tensor_tensor(e, e, over_nodes(gam), ALU.mult))
                    chain.step(nc.vector.tensor_tensor(e, e, over_nodes(bet), ALU.add))
                    chain.step(nc.vector.tensor_tensor(e, e, R[:, of(m), :], ALU.add))
                    chain.step(nc.vector.tensor_tensor(x, x, e, ALU.add))
                    centre(("x", m), x, m, e)
                if 0 <= i - 3 < NB:
                    variance(("x", i - 3), cen[(i - 3) % 2][:, :, :], i - 3)
                if 0 <= i - 4 < NB:
                    m = i - 4
                    relu_norm(("x", m), E[:, of(m), :], m, R[:, of(m), :]).then_inc(rows_ready, 1)
                if 0 <= i - 5 < NB:
                    m = i - 5
                    dve.wait_ge(upper_ready, m + 1)
                    nc.vector.tensor_tensor(feats[0][:, of(m), D:2 * D], R[:, of(m), :],
                                            feats[0][:, of(m), 0:D].bitcast(F32), ALU.subtract).then_inc(feats_ready, 1)

            def take_rest(r):
                p, m = plan.rows[r]
                dve.wait_ge(upper_ready, NB + r + 1)
                nc.vector.tensor_tensor(feats[(p + 1) % 2][:, of(m), D:2 * D], MADE[p][:, of(m), :],
                                        feats[(p + 1) % 2][:, of(m), 0:D].bitcast(F32), ALU.subtract).then_inc(feats_ready, 1)

            for s in range(N_STEPS):
                n = plan.step_tile[s]
                if n is not None:
                    slot = n % SLOTS
                    dve.wait_ge(high_ready, TOTAL_TILES + n + 1)
                    nc.vector.tensor_tensor(low[slot][:, :, :], whole[slot][:, :, :], high[slot][:, :, :].bitcast(F32),
                                            ALU.subtract).then_inc(low_ready, 1)
                for r in plan.rows_at(s, 10, 3):
                    take_rest(r)
                for r in plan.rows_at(s, 9, 3):
                    p, m = plan.rows[r]
                    dve.wait_ge(feat_mult, plan.weigh_no[r, 1] + 1)
                    g = E[:, of(m), :]
                    nc.vector.tensor_tensor(g, weighed, over_nodes(b3), ALU.add).then_inc(mult_read, 1)
                    dve.wait_ge(mult_read, plan.weigh_no[r, 1] + 1)
                    dve.wait_ge(dis_ready, 1)
                    nc.vector.tensor_tensor(g, g, over_features(dis[:, of(m)]), ALU.mult).then_inc(rows_ready, 1)
                for r in plan.rows_at(s, 7, 3):
                    p, m = plan.rows[r]
                    relu_norm((p, m), cen[r % 2][:, :, :], m, R[:, of(m), :]).then_inc(rows_ready, 1)
                for r in plan.rows_at(s, 6, 3):
                    variance(plan.rows[r], sq[r % 2][:, :, :], plan.rows[r][1])
                for r, j in plan.turns_at(s, 2):
                    p, m = plan.rows[r]
                    if j == 0:
                        q = plan.weigh_no[r, j]
                        dve.wait_ge(feat_mult, q + 1)
                        nc.vector.tensor_tensor(X[:, of(m), :], weighed, X[:, of(m), :], ALU.add).then_inc(mult_read, 1)
                        dve.wait_ge(mult_read, q + 1)
                        if p == 3:
                            centre((p, m), X[:, of(m), :], m, cen[r % 2][:, :, :])
                for r in plan.rows_at(s, 5, 0):
                    take_rest(r)
                for r in plan.rows_at(s, 4, 0):
                    p, m = plan.rows[r]
                    relu_norm((p, m), cen[r % 2][:, :, :], m, E[:, of(m), :]).then_inc(rows_ready, 1)
                    chain.step(nc.vector.tensor_tensor(X[:, of(m), :], X[:, of(m), :], over_nodes(b2), ALU.add))
                for r in plan.rows_at(s, 3, 0):
                    variance(plan.rows[r], sq[r % 2][:, :, :], plan.rows[r][1])
                for r in plan.rows_at(s, 3, 1):
                    m = plan.rows[r][1]
                    dve.wait_ge(upper_ready, NB + r + 1)
                    nc.vector.tensor_tensor(feats[0][:, of(m), D:2 * D], aux_rows[0],
                                            feats[0][:, of(m), 0:D].bitcast(F32), ALU.subtract).then_inc(feats_ready, 1)
                for r in plan.rows_at(s, 3, 2):
                    take_rest(r)
                for r in plan.rows_at(s, 2, *range(PASSES)):
                    p, m = plan.rows[r]
                    if p == 1:
                        continue
                    dve.wait_ge(y_rows, r + 1)
                    if p == 0:
                        x = X[:, of(m), :]
                        nc.vector.tensor_tensor(x, aux_rows[0], x, ALU.add).then_inc(y_read, 1)
                        dve.wait_ge(y_read, r + 1)
                        centre((p, m), x, m, cen[r % 2][:, :, :])
                    elif p in (2, 3):
                        v = E if p == 2 else R
                        stt(v[:, of(m), :], aux_rows[0], 2.0, v[:, of(m), :], ALU.mult, ALU.subtract).then_inc(rows_ready, 1)
                    else:
                        i = r - 4 * NB
                        o = cen[r % 2][:, :, :]
                        nc.vector.tensor_tensor(o, aux_rows[0], E[:, of(m), :], ALU.add).then_inc(y_read, 1)
                        dve.wait_ge(y_read, NB + i + 1)
                        chain.step(stt(o, o, 0.0, over_features(dis[:, of(m)]), ALU.max, ALU.mult))
                        if i >= 2:
                            dve.wait_ge(out_stored[i % 2], 16 * (i // 2))
                        nc.vector.tensor_tensor(out_rows[i % 2][:, :, :], o, X[:, of(m), :], ALU.add).then_inc(out_ready, 1)
                for r in plan.rows_at(s, 1, *range(PASSES)):
                    p, m = plan.rows[r]
                    dve.wait_ge(multiplied, plan.own_no[plan.last_own[p, m]])
                    if r >= 2:
                        dve.wait_ge(y_rows, r - 1)
                    if (p, m) in DUAL_NO:
                        dve.wait_ge(part_saved, DUAL_NO[p, m] + 1)
                        ins = nc.vector.tensor_tensor(y_sb[r % 2][:, :], own_bank[r % OWN_BANKS], part[:, m, :], ALU.add)
                    else:
                        ins = nc.vector.tensor_copy(y_sb[r % 2][:, :], own_bank[r % OWN_BANKS])
                    ins.then_inc(y_saved, 1)

        @block.gpsimd
        def _(pool):
            op = nc.gpsimd
            chain = Chain(pool, pool_step)
            chain.step(op.memset(minus_half[:, :], -0.5))
            chain.step(op.memset(ident[:, :], 0.0))
            chain.step(op.memset(fold[:, :], 0.0))
            op.affine_select(out=ident[:, :], in_=ident[:, :], compare_op=ALU.not_equal, fill=1.0, base=0,
                             pattern=[[-1, P]], channel_multiplier=1).then_inc(made, 1)
            op.affine_select(out=fold[:, :], in_=fold[:, :], compare_op=ALU.not_equal, fill=1.0, base=0,
                             pattern=[[-1, D]], channel_multiplier=1).then_inc(made, 1)
            pool.wait_ge(made, 2)
            op.affine_select(out=fold[:, :], in_=fold[:, :], compare_op=ALU.not_equal, fill=1.0, base=-D,
                             pattern=[[-1, D]], channel_multiplier=1).then_inc(made, 1)

            def raise_variances(rows):
                for row in rows:
                    pool.wait_ge(var_ready, LN_NO[row] + 1)
                    v = rstd[:, of(row[1])]
                    op.tensor_tensor(v, v, minus_half[:, 0:SUB], ALU.pow).then_inc(pow_ready, 1)

            raise_variances(LN_START)
            raise_variances(LN_H)
            pool.wait_ge(deg_ready, 1)
            chain.step(op.tensor_scalar(dis[:, :], dis[:, :], 1.0, None, ALU.add))
            chain.step(op.tensor_scalar(diag[:, :], dis[:, :], 0.0, None, ALU.is_equal))
            chain.step(op.tensor_tensor(dis[:, :], dis[:, :], diag[:, :], ALU.add))
            chain.step(op.tensor_tensor(dis[:, :], dis[:, :], minus_half[:, :], ALU.pow))
            chain.step(op.tensor_scalar(diag[:, :], diag[:, :], -1.0, 1.0, ALU.mult, ALU.add))
            op.tensor_tensor(dis[:, :], dis[:, :], diag[:, :], ALU.mult).then_inc(dis_ready, 1)
            raise_variances(LN_PASS)


_INS = ['x', 'adj', 'L0_gnn_W_u', 'L0_gnn_diag_u', 'L0_gnn_par_u', 'L0_gnn_W_i', 'L0_gnn_diag_i', 'L0_gnn_par_i',
        'L0_gnn_ln_gamma', 'L0_gnn_ln_beta', 'L2_gnn_weights', 'L2_gnn_bias', 'L3_gnn_W', 'L3_gnn_b']


def kernel(**inputs):
    import numpy as _np
    import concourse.bacc as _bacc
    from concourse import mybir as _mybir
    from concourse.bass_utils import run_bass_kernel_spmd as _run

    nc = _bacc.Bacc("TRN2", target_bir_lowering=False, num_devices=1)
    arrays, args = {}, []
    for name in _INS:
        a = _np.ascontiguousarray(inputs[name])
        arrays[f"in_{name}_dram"] = a
        args.append(nc.dram_tensor(f"in_{name}_dram", a.shape, _mybir.dt.from_np(a.dtype), kind="ExternalInput").ap())
    out = nc.dram_tensor("out_dram", (N, D), _mybir.dt.float32, kind="ExternalOutput").ap()
    gnn_stack(nc, *args, out)
    r = _run(nc, [arrays], core_ids=[0])
    return r.results[0]["out_dram"]
```

```python
import concourse.bass as bass
from concourse import mybir
from contextlib import ExitStack
import numpy as np

F32 = mybir.dt.float32
F32R = mybir.dt.float32r
ALU = mybir.AluOpType
ACT = mybir.ActivationFunctionType
AX = mybir.AxisListType

P = 128
N = 5120
D = 64
U = 2048
B = 512
SUB = B // P
NB = N // B
NT = N // P
HALVES = 2
HS = SUB // HALVES
PASSES = 5
SLOTS = 4
LAG = 2
OWN_BANKS = 3
DUAL_BANKS = 2
EPS = 1e-5
RD = SUB * D



class Chain:

    def __init__(self, eng, sem):
        self.eng, self.sem, self.n = eng, sem, 0

    def step(self, ins):
        ins.then_inc(self.sem, 1)
        self.n += 1
        self.eng.wait_ge(self.sem, self.n)


WEIGH = [5, None, None, 4, None]
NORM = [3, None, None, 3, None]
MAKE = [(NORM[0] + 1,), (), (2,), (NORM[3] + 1, WEIGH[3] + 2), ()]
SPLIT = [5, 2, 3, 7, None]


class Plan:

    def __init__(self):
        self.tiles = []
        self.step_tile = []
        self.rows = []
        self.ended = {}
        self.row_no = {}
        self.end_step = {}
        self.duals_in = {}
        self.first_own, self.last_own, self.first_dual, self.last_dual = {}, {}, {}, {}
        self.dual_rows = []
        ready = {(0, m): 0 for m in range(NB)}
        turns = set()
        covered = {(0, m): set() for m in range(NB)}
        for p in range(PASSES):
            order = list(range(NB)) if p % 2 == 0 else list(range(NB))[::-1]
            cols = {m: [k for k in order if k not in covered[p, m]] for m in order}
            late = order[0] if p else None
            seq = []
            head = order[:OWN_BANKS if p + 1 < PASSES else OWN_BANKS + DUAL_BANKS] if p else []
            seq += [(m, k) for m in head for k in cols[m] if k != late]
            seq += [(m, k) for m in head for k in cols[m] if k == late]
            seq += [(m, k) for m in order if m not in head for k in cols[m]]
            left = {m: len(cols[m]) for m in order}
            for m in order:
                covered[p + 1, m] = set()
            for m, k in seq:
                while ready[p, k] > len(self.step_tile) or \
                        left[m] == 1 and WEIGH[p] and len(self.step_tile) + WEIGH[p] in turns:
                    self.step_tile.append(None)
                step, n = len(self.step_tile), len(self.tiles)
                dual = p + 1 < PASSES and ready.get((p + 1, k), 1 << 30) <= step + LAG
                self.step_tile.append(n)
                self.tiles.append((p, m, k, dual))
                self.first_own.setdefault((p, m), n)
                self.last_own[p, m] = n
                if dual:
                    covered[p + 1, m].add(k)
                    self.duals_in.setdefault(max(step, ready[p + 1, k]), []).append(n)
                left[m] -= 1
                if left[m] == 0:
                    if WEIGH[p]:
                        turns.add(step + WEIGH[p])
                    self.row_no[p, m] = len(self.rows)
                    self.end_step[p, m] = step
                    self.ended.setdefault(step, []).append(len(self.rows))
                    self.rows.append((p, m))
                    if SPLIT[p] is not None:
                        ready[p + 1, m] = step + SPLIT[p]
        self.step_tile += [None] * 6
        self.steps = len(self.step_tile)
        turns = sorted((self.end_step[p, m] + WEIGH[p], self.row_no[p, m]) for (p, m) in self.rows if WEIGH[p])
        self.weigh_no = {r: q for q, (_, r) in enumerate(turns)}
        self.own_no, self.dual_no, count = {}, {}, 0
        last_dual_step = {}
        for s, n in enumerate(self.step_tile):
            if n is not None:
                count += 1
                self.own_no[n] = count
            for n in self.duals_in.get(s, []):
                count += 1
                self.dual_no[n] = count
                p, m, k, _ = self.tiles[n]
                if (p + 1, m) not in self.first_dual:
                    self.first_dual[p + 1, m] = n
                    self.dual_rows.append((p + 1, m))
                self.last_dual[p + 1, m] = n
                last_dual_step[p + 1, m] = s
        events = sorted((self.end_step[p, m] + d, -d, self.row_no[p, m], j)
                        for (p, m) in self.rows for j, d in enumerate(MAKE[p]))
        self.made_no = {(r, j): i + 1 for i, (_, _, r, j) in enumerate(events)}
        self.part_saved_in = {}
        for i, row in enumerate(self.dual_rows):
            p, m = row
            s = max(last_dual_step[row], self.end_step[p - 1, m]) + 2
            self.part_saved_in.setdefault(s, []).append(i)

    def bank(self, r):
        i = r - NB * (PASSES - 1)
        return r % OWN_BANKS if i < 0 else [1, 2, 0, 3, 4][i % (OWN_BANKS + DUAL_BANKS)]

    def used_no(self, n):
        return self.dual_no.get(n, self.own_no[n])

    def rows_at(self, step, delay, *passes):
        return [r for r in self.ended.get(step - delay, []) if self.rows[r][0] in passes]

    def turns_at(self, step, delay=0):
        return [r for r, (p, m) in enumerate(self.rows) if WEIGH[p] and self.end_step[p, m] + WEIGH[p] == step - delay]


def gnn_stack(nc, x_d, adj_d, wu_d, du_d, pu_d, wi_d, di_d, pi_d, gam_d, bet_d, w2_d, b2_d, w3_d, b3_d, out_d):
    plan = Plan()
    ctx = ExitStack()
    with ctx:
        def sb(name, shape, dt=F32, stack=ctx):
            return stack.enter_context(nc.sbuf_tensor(name, shape, dt))

        def sem(name):
            return ctx.enter_context(nc.semaphore(name))

        adj_t = nc.dram_tensor("adj_t", (NB, NB, P, SUB, B), F32, kind="Internal").ap()

        whole = [sb(f"whole{s}", [P, SUB, B]) for s in range(2)]
        high = [sb(f"high{s}", [P, SUB, B], F32R) for s in range(2)]
        low = [sb(f"low{s}", [P, SUB, B], F32R) for s in range(2)]
        X = sb("X", [P, NT, D])
        E = sb("E", [P, NT, D])
        R = sb("R", [P, NT, D])
        t_cur = sb("t_cur", [P, SUB, 2 * D], F32R)
        deg_part = sb("deg_part", [P, NT, NB])
        dis = sb("dis", [P, NT])
        diag = sb("diag", [P, NT])
        par = sb("par", [P, 4])
        total = sb("total", [P, NT])
        rstd = sb("rstd", [P, NT])
        minus_half = sb("minus_half", [P, NT])
        gam = sb("gam", [P, D])
        bet = sb("bet", [P, D])
        b2 = sb("b2", [P, D])
        b3 = sb("b3", [P, D])
        w_in = sb("w_in", [D, 2, D])
        w0 = sb("w0", [D, D])
        fold_weigh = sb("fold_weigh", [P, 3, 2 * D])
        w3 = sb("w3", [D, D])
        ident = sb("ident", [P, P])
        fold = sb("fold", [P, D])
        fold_centred = sb("fold_centred", [P, D])
        cen = [sb(f"cen{i}", [P, SUB, D]) for i in range(2)]
        sq = [sb(f"sq{i}", [P, SUB, D]) for i in range(2)]
        with ExitStack() as early:
            raw = sb("raw", [P, NB, SUB, B], F32, early)
            h_acc = sb("h_acc", [P, NB, B], F32, early)
            S = sb("S", [P, NT, D], F32, early)
            ego_t = [sb(f"ego_t{i}", [D, B], F32, early) for i in range(2)]
        feats = [sb("feats0", [P, NT, 2 * D], F32R)]
        whole += [sb(f"whole{s}", [P, SUB, B]) for s in range(2, SLOTS)]
        high += [sb(f"high{s}", [P, SUB, B], F32R) for s in range(2, SLOTS)]
        low += [sb(f"low{s}", [P, SUB, B], F32R) for s in range(2, SLOTS)]
        feats.append(sb("feats1", [P, NT, 2 * D], F32R))
        part = sb("part", [P, NB, B])
        y_sb = [sb(f"y_sb{i}", [P, B]) for i in range(2)]
        feat_t = [sb(f"feat_t{i}", [D, B]) for i in range(2)]
        out_rows = sq

        turned = [ctx.enter_context(nc.psum_tensor(f"turned{h}", [P, HS, B], F32)) for h in range(HALVES)]
        acc = [ctx.enter_context(nc.psum_tensor(f"acc{i}", [P, B], F32)) for i in range(2)]
        aux = [ctx.enter_context(nc.psum_tensor(f"aux{i}", [P, B], F32)) for i in range(2)]
        dual_bank = [turned[1][:, 0, :], turned[1][:, 1, :]]
        own_bank = [acc[0][:, :], acc[1][:, :], turned[0][:, 0, :]] + dual_bank
        weighed = turned[0][:, 1, 0:RD].rearrange("p (a d) -> p a d", d=D)
        aux_rows = [a[:, 0:RD].rearrange("p (a d) -> p a d", d=D) for a in aux]

        raw_in = [sem(f"raw_in{s}") for s in range(NB)]
        whole_in = [sem(f"whole_in{s}") for s in range(SLOTS)]
        stored = [sem(f"stored{s}") for s in range(2)]
        early_in = sem("early_in")
        late_in = sem("late_in")
        weights_ready = sem("weights_ready")
        x_in = sem("x_in")
        made = sem("made")
        half_turned = sem("half_turned")
        half_copied = sem("half_copied")
        high_ready = sem("high_ready")
        low_ready = sem("low_ready")
        used = sem("used")
        deg_summed = sem("deg_summed")
        h_added = sem("h_added")
        t_done = sem("t_done")
        t_copied = sem("t_copied")
        t_turned = sem("t_turned")
        t_high = sem("t_high")
        t_ready = sem("t_ready")
        centred = sem("centred")
        squared = sem("squared")
        var_ready = sem("var_ready")
        pow_ready = sem("pow_ready")
        ego_ready = sem("ego_ready")
        ego_turned = sem("ego_turned")
        ego_copied = sem("ego_copied")
        ego_mult = sem("ego_mult")
        e_ready = sem("e_ready")
        h_rows = sem("h_rows")
        multiplied = sem("multiplied")
        part_saved = sem("part_saved")
        y_saved = sem("y_saved")
        y_rows = sem("y_rows")
        y_read = sem("y_read")
        rows_ready = sem("rows_ready")
        upper_ready = sem("upper_ready")
        feats_ready = sem("feats_ready")
        feat_turned = sem("feat_turned")
        feat_copied = sem("feat_copied")
        feat_mult = sem("feat_mult")
        mult_read = sem("mult_read")
        x_ready = sem("x_ready")
        deg_ready = sem("deg_ready")
        dis_ready = sem("dis_ready")
        out_ready = sem("out_ready")
        out_stored = [sem(f"out_stored{i}") for i in range(2)]
        dve_step = sem("dve_step")
        pool_step = sem("pool_step")

        adj_v = adj_d.rearrange("(m a p) (g k) -> p m a g k", a=SUB, p=P, k=B)
        x_v = x_d.rearrange("(t p) d -> p t d", p=P)
        out_v = out_d.rearrange("(m a p) d -> p m a d", a=SUB, p=P)
        adj_t_v = adj_t.rearrange("m k p a n -> p m k (a n)")
        WEIGHTS = {0: w0, 3: w3}
        SOURCE = {0: E, 3: R}
        MADE = {0: E, 2: E, 3: E}
        LN_START = [("start", m) for m in range(NB)]
        LN_H = [x for i in range(NB + 3) for x in ((("h", i),) if i < NB else ()) + ((("x", i - 3),) if i >= 3 else ())]
        LN_PASS = [(p, m) for p, m in plan.rows if p in (0, 3)]
        LN_NO = {x: i for i, x in enumerate(LN_START + LN_H + LN_PASS)}
        CENTRED_NO = {x: i for i, x in enumerate([x for x in LN_START + LN_H + LN_PASS if x[0] != "h"])}

        def features_made(r, j):
            return NB + plan.made_no[r, j]

        def of(m):
            return slice(m * SUB, (m + 1) * SUB)

        row_shape = [P, SUB, D]
        y_wide = aux[0][:, :].rearrange("p (a c) -> p a c", c=2 * D)
        y_part, y_weighed = y_wide[:, :, 0:D], y_wide[:, :, D:2 * D]
        ego_turning = turned[0][0:D, 0, :]
        ego_product = turned[1][:, 0, 0:RD].rearrange("p (a d) -> p a d", d=D)
        t_t = ego_t[0]

        def over_features(v):
            return v.unsqueeze(2).broadcast_to(row_shape)

        def over_nodes(v):
            return v[:, :].unsqueeze(1).broadcast_to(row_shape)

        N_STEPS = plan.steps
        END_STAGES = NB + 7
        DUAL_NO = {row: i for i, row in enumerate(plan.dual_rows)}
        TOTAL_TILES = NB * NB

        block = ctx.enter_context(nc.Block())

        @block.sync
        def _(sp):
            sp.dma_start(X[:, :, :], x_v).then_inc(x_in, 16)
            for dst, src in ((diag[:, 0:U // P], du_d.rearrange("(t p) -> p t", p=P)),
                             (diag[:, U // P:NT], di_d.rearrange("(t p) -> p t", p=P)),
                             (par[:, 0:2], pu_d.partition_broadcast(P)), (par[:, 2:4], pi_d.partition_broadcast(P)),
                             (w_in[:, 0, :], wu_d), (w_in[:, 1, :], wi_d)):
                sp.dma_start(dst, src, allow_slow_non_contiguous=True).then_inc(early_in, 16)
            for m in range(NB):
                sp.dma_start(raw[:, m], adj_v[:, m, :, 0, :]).then_inc(raw_in[m], 16)

            def store(g, m):
                sp.wait_ge(half_copied, g * (NB * 2) + (2 * m + 2))
                src = whole[m % 2][:, :, :].rearrange("p a n -> p (a n)")
                dst = adj_t_v[:, m, g] if isinstance(g, int) else \
                    adj_t_v[:, m, bass.ds(g, 1), :].rearrange("p g n -> p (g n)")
                sp.dma_start(dst, src).then_inc(stored[m % 2], 16)

            def load_next(g, m):
                sp.wait_ge(half_turned, g * (NB * 2) + (2 * m + 2))
                src = adj_v[:, m, :, g + 1, :] if isinstance(g, int) else \
                    adj_v[:, m, :, bass.ds(g + 1, 1), :].rearrange("p a g k -> p a (g k)")
                sp.dma_start(raw[:, m], src).then_inc(raw_in[m], 16)

            def group(g):
                for m in range(NB):
                    load_next(g, m)
                    store(g, m)

            group(0)
            with sp.Fori(1, NB - 1) as g:
                group(g)
            for m in range(NB):
                store(NB - 1, m)
            for s in range(2):
                sp.wait_ge(stored[s], 16 * TOTAL_TILES // 2)
            for n, (p, m, k, dual) in enumerate(plan.tiles):
                if n >= SLOTS:
                    sp.wait_ge(low_ready, TOTAL_TILES + n - SLOTS + 1)
                elif n < 2:
                    sp.wait_ge(low_ready, TOTAL_TILES)
                sp.dma_start(whole[n % SLOTS][:, :, :].rearrange("p a n -> p (a n)"), adj_t_v[:, m, k]) \
                    .then_inc(whole_in[n % SLOTS], 16)

        @block.tensor
        def _(pe):
            def multiply(v, slot, bank, start, stop):
                for i in range(SUB):
                    for piece in (high, low):
                        last = nc.tensor.matmul(bank, v[:, i, :], piece[slot][:, i, :],
                                                start=start and i == 0 and piece is high,
                                                stop=stop and i == SUB - 1 and piece is low)
                return last

            def products_for_t(g, m):
                pe.wait_ge(raw_in[m], g * 16 + 16)
                for a in range(SUB):
                    last = nc.tensor.matmul(aux[0][0:D, :], E[:, m * SUB + a, :], raw[:, m, a, :],
                                            start=(m == 0 and a == 0), stop=(m == NB - 1 and a == SUB - 1))
                if m == NB - 1:
                    last.then_inc(t_done, 1)

            pe.wait_ge(made, 4)
            for m in range(NB + 2):
                if m < NB:
                    pe.wait_ge(ego_ready, m + 1)
                    if m >= 1:
                        pe.wait_ge(ego_copied, m)
                    for a in range(SUB):
                        last = nc.tensor.transpose(ego_turning[:, a * P:(a + 1) * P], S[:, m * SUB + a, :], ident[:, :])
                    last.then_inc(ego_turned, 1)
                if 1 <= m <= NB:
                    r = m - 1
                    if r == 0:
                        pe.wait_ge(early_in, 16 * 6)
                    pe.wait_ge(ego_copied, r + 1)
                    if r >= 1:
                        pe.wait_ge(e_ready, r)
                    for a in range(SUB):
                        last = nc.tensor.matmul(ego_product[:, a, :], ego_t[r % 2][:, a * P:(a + 1) * P],
                                                w_in[:, 0 if r * B < U else 1, :], start=True, stop=True)
                    last.then_inc(ego_mult, 1)
                if m >= 2:
                    pe.wait_ge(e_ready, m - 1)
                    products_for_t(0, m - 2)

            def turn_half(g, m, h):
                if not (isinstance(g, int) and g * NB + m == 0):
                    pe.wait_ge(half_copied, g * (NB * 2) + (2 * m + h - 1))
                for b in range(HS):
                    for a in range(SUB):
                        last = nc.tensor.transpose(turned[h][:, b, a * P:(a + 1) * P],
                                                   raw[:, m % NB, a, (h * HS + b) * P:(h * HS + b + 1) * P], ident[:, :])
                last.then_inc(half_turned, 1)

            def turn_t(g):
                pe.wait_ge(t_copied, g + 1)
                for b in range(SUB):
                    last = nc.tensor.matmul(aux[1][:, b * D:(b + 1) * D], t_t[:, b * P:(b + 1) * P], ident[0:D, 0:D],
                                            start=True, stop=True)
                last.then_inc(t_turned, 1)

            def end_of_layer(i):
                if i < NB:
                    pe.wait_ge(h_added, TOTAL_TILES - NB + i + 1)
                    if i >= 2:
                        pe.wait_ge(squared, LN_NO["h", i - 2] + 1)
                    for a in range(SUB):
                        last = nc.tensor.matmul(aux[i % 2][:, a * D:(a + 1) * D], h_acc[:, i, a * P:(a + 1) * P],
                                                fold_centred[:, :], start=True, stop=True)
                    last.then_inc(h_rows, 1)
                if i == NB:
                    pe.wait_ge(squared, LN_NO["h", NB - 1] + 1)

            def group(g, followed=True):
                first = isinstance(g, int) and g == 0
                for m in range(NB):
                    if m + 1 < NB or followed:
                        pe.wait_ge(deg_summed, g * NB + (m + 2))
                        turn_half(g, m + 1, 0)
                        if m == 0:
                            turn_t(g)
                        turn_half(g, m + 1, 1)
                    if m == 0:
                        pe.wait_ge(t_ready, g + 1)
                    pe.wait_ge(low_ready, g * NB + (m + 1))
                    if not (first and m < 2):
                        pe.wait_ge(h_added, g * NB + (m - 1))
                    multiply(t_cur, m % 2, acc[m % 2][:, :], True, True).then_inc(used, 1)
                    if followed:
                        products_for_t(g + 1, m)
                    elif m >= 1:
                        end_of_layer(m - 1)

            pe.wait_ge(e_ready, NB)
            pe.wait_ge(deg_summed, 1)
            for h in range(HALVES):
                turn_half(0, 0, h)
            group(0)
            with pe.Fori(1, NB - 1) as g:
                group(g)
            group(NB - 1, followed=False)

            for s in range(N_STEPS):
                if NB - 1 + s < END_STAGES:
                    end_of_layer(NB - 1 + s)
                n = plan.step_tile[s]
                if n is not None:
                    p, m, k, dual = plan.tiles[n]
                    pe.wait_ge(low_ready, TOTAL_TILES + n + 1)
                    pe.wait_ge(feats_ready, k + 1 if p == 0 else NB + plan.row_no[p - 1, k] + 1)
                    first, last_one = plan.first_own[p, m] == n, plan.last_own[p, m] == n
                    number = NB * p + (m if p % 2 == 0 else NB - 1 - m)
                    if first:
                        before = [r for r in range(number) if plan.bank(r) == plan.bank(number)]
                        if before:
                            pe.wait_ge(y_saved, before[-1] + 1)
                        elif plan.bank(number) >= OWN_BANKS:
                            pe.wait_ge(part_saved, len(plan.dual_rows))
                    multiply(feats[p % 2][:, of(k)], n % SLOTS, own_bank[plan.bank(number)], first, last_one) \
                        .then_inc(multiplied, 1)
                for r in plan.rows_at(s, 1, *range(PASSES)):
                    pe.wait_ge(y_saved, r + 1)
                    p = plan.rows[r][0]
                    if r >= 1:
                        pe.wait_ge(y_read, r)
                    if r == NB:
                        pe.wait_ge(weights_ready, 1)
                    for a in range(SUB):
                        turned_y = y_sb[r % 2][:, a * P:(a + 1) * P]
                        if p in (1, 2, 3):
                            last = nc.tensor.matmul(y_wide[:, a, :], turned_y, fold_weigh[:, p - 1, :], start=True, stop=True)
                        else:
                            last = nc.tensor.matmul(aux_rows[0][:, a, :], turned_y, fold[:, :], start=True, stop=True)
                    last.then_inc(y_rows, 1)
                for r in plan.turns_at(s):
                    q, (p, m) = plan.weigh_no[r], plan.rows[r]
                    pe.wait_ge(rows_ready, features_made(r, 0))
                    if q >= 1:
                        pe.wait_ge(feat_copied, q)
                    for a in range(SUB):
                        last = nc.tensor.transpose(aux[1][0:D, a * P:(a + 1) * P], SOURCE[p][:, m * SUB + a, :], ident[:, :])
                    last.then_inc(feat_turned, 1)
                for r in plan.turns_at(s, 1):
                    q, (p, m) = plan.weigh_no[r], plan.rows[r]
                    pe.wait_ge(feat_copied, q + 1)
                    if q == 0:
                        pe.wait_ge(weights_ready, 1)
                    else:
                        pe.wait_ge(mult_read, q)
                    for a in range(SUB):
                        last = nc.tensor.matmul(weighed[:, a, :], feat_t[q % 2][:, a * P:(a + 1) * P], WEIGHTS[p][:, :],
                                                start=True, stop=True)
                    last.then_inc(feat_mult, 1)
                for n in plan.duals_in.get(s, []):
                    p, m, k, _ = plan.tiles[n]
                    row = (p + 1, m)
                    i = DUAL_NO[row]
                    pe.wait_ge(feats_ready, NB + plan.row_no[p, k] + 1)
                    first, last_one = plan.first_dual[row] == n, plan.last_dual[row] == n
                    if first and i >= 2:
                        pe.wait_ge(part_saved, i - 1)
                    multiply(feats[(p + 1) % 2][:, of(k)], n % SLOTS, dual_bank[i % 2], first, last_one) \
                        .then_inc(multiplied, 1)

        @block.scalar
        def _(act):
            def square(row, v, out):
                if row[0] == "h":
                    act.wait_ge(h_rows, row[1] + 1)
                else:
                    act.wait_ge(centred, CENTRED_NO[row] + 1)
                nc.scalar.activation(out, v, ACT.Square).then_inc(squared, 1)

            def copy_ego(m):
                act.wait_ge(ego_turned, m + 1)
                if m >= 2:
                    act.wait_ge(ego_mult, m - 1)
                nc.scalar.activation(ego_t[m % 2][:, :], ego_turning, ACT.Copy).then_inc(ego_copied, 1)

            for m in range(NB + 2):
                if m < NB:
                    square(("start", m), R[:, of(m), :], sq[m % 2][:, :, :])
                if m >= 2:
                    copy_ego(m - 2)
            w123_v = w2_d[1:4].rearrange("k i o -> i k o")
            for dst, src in ((w3[:, :], w3_d), (w0[:, :], w2_d[0]),
                             (fold_weigh[0:D, :, D:2 * D], w123_v), (fold_weigh[D:2 * D, :, D:2 * D], w123_v),
                             (gam[:, :], gam_d.partition_broadcast(P)), (bet[:, :], bet_d.partition_broadcast(P)),
                             (b2[:, :], b2_d.partition_broadcast(P)), (b3[:, :], b3_d.partition_broadcast(P))):
                act.dma_start(dst, src).then_inc(late_in, 16)

            def copy_turned(g, m):
                for h in range(HALVES):
                    act.wait_ge(half_turned, g * (NB * 2) + (2 * m + h + 1))
                    if h == 0 and not (isinstance(g, int) and g * NB + m < 2):
                        act.wait_ge(stored[m % 2], g * (16 * NB // 2) + 16 * (m // 2))
                        act.wait_ge(low_ready, g * NB + (m - 1))
                    nc.scalar.activation(whole[m % 2][:, h * HS:(h + 1) * HS, :], turned[h][:, :, :],
                                         ACT.Copy).then_inc(half_copied, 1)

            def take_high(g, m):
                act.wait_ge(half_copied, g * (NB * 2) + (2 * m + 2))
                if not (isinstance(g, int) and g * NB + m < 2):
                    act.wait_ge(used, g * NB + (m - 1))
                nc.scalar.activation(high[m % 2][:, :, :], whole[m % 2][:, :, :], ACT.Copy).then_inc(high_ready, 1)

            def copy_t(g):
                act.wait_ge(t_done, g + 1)
                if not isinstance(g, int) or g > 0:
                    act.wait_ge(t_turned, g)
                nc.scalar.activation(t_t[:, :], aux[0][0:D, :], ACT.Copy).then_inc(t_copied, 1)

            def take_t_high(g):
                act.wait_ge(t_turned, g + 1)
                if not isinstance(g, int) or g > 0:
                    act.wait_ge(used, g * NB)
                nc.scalar.activation(t_cur[:, :, 0:D], aux_rows[1], ACT.Copy).then_inc(t_high, 1)

            def end_of_layer(i):
                if i < NB:
                    act.wait_ge(h_rows, i + 1)
                    nc.scalar.activation(E[:, of(i), :], aux_rows[i % 2], ACT.Copy)
                    if i >= 2:
                        act.wait_ge(var_ready, LN_NO["h", i - 2] + 1)
                    square(("h", i), aux_rows[i % 2], sq[i % 2][:, :, :])
                if 0 <= i - 3 < NB:
                    m = i - 3
                    if m >= 2:
                        act.wait_ge(var_ready, LN_NO["x", m - 2] + 1)
                    square(("x", m), E[:, of(m), :], cen[m % 2][:, :, :])
                if 0 <= i - 6 < NB:
                    m = i - 6
                    act.wait_ge(rows_ready, m + 1)
                    nc.scalar.activation(feats[0][:, of(m), 0:D], R[:, of(m), :], ACT.Copy).then_inc(upper_ready, 1)

            def group(g, followed=True):
                take_t_high(g)
                for m in range(1, NB + 1):
                    if m < NB or followed:
                        copy_turned(g, m)
                        take_high(g, m)
                    if not followed and m >= 2:
                        end_of_layer(m - 2)
                if followed:
                    copy_t(g + 1)

            copy_t(0)
            copy_turned(0, 0)
            take_high(0, 0)
            group(0)
            with act.Fori(1, NB - 1) as g:
                group(g)
            group(NB - 1, followed=False)

            for s in range(N_STEPS):
                n = plan.step_tile[s]
                if n is not None:
                    slot = n % SLOTS
                    act.wait_ge(whole_in[slot], 16 * (n // SLOTS + 1))
                    if n >= SLOTS:
                        act.wait_ge(multiplied, plan.used_no(n - SLOTS))
                    nc.scalar.activation(high[slot][:, :, :], whole[slot][:, :, :], ACT.Copy).then_inc(high_ready, 1)
                if NB - 1 + s < END_STAGES:
                    end_of_layer(NB - 1 + s)
                for i in plan.part_saved_in.get(s, []):
                    p, m = plan.dual_rows[i]
                    act.wait_ge(multiplied, plan.dual_no[plan.last_dual[p, m]])
                    act.wait_ge(y_saved, plan.row_no[p - 1, m] + 1)
                    nc.scalar.activation(part[:, m, :], dual_bank[i % 2], ACT.Copy).then_inc(part_saved, 1)
                for r in plan.rows_at(s, SPLIT[1], 1):
                    p, m = plan.rows[r]
                    act.wait_ge(y_rows, r + 1)
                    nc.scalar.activation(feats[0][:, of(m), 0:D], y_part, ACT.Copy).then_inc(upper_ready, 1)
                for r in plan.rows_at(s, NORM[0], 0) + plan.rows_at(s, NORM[3], 3):
                    square(plan.rows[r], cen[r % 2][:, :, :], sq[r % 2][:, :, :])
                for r in plan.rows_at(s, SPLIT[0], 0) + plan.rows_at(s, SPLIT[2], 2) + plan.rows_at(s, SPLIT[3], 3):
                    p, m = plan.rows[r]
                    act.wait_ge(rows_ready, features_made(r, len(MAKE[p]) - 1))
                    nc.scalar.activation(feats[(p + 1) % 2][:, of(m), 0:D], MADE[p][:, of(m), :], ACT.Copy).then_inc(upper_ready, 1)
                for r in plan.turns_at(s, 2):
                    q = plan.weigh_no[r]
                    act.wait_ge(feat_turned, q + 1)
                    if q >= 2:
                        act.wait_ge(feat_mult, q - 1)
                    nc.scalar.activation(feat_t[q % 2][:, :], aux[1][0:D, :], ACT.Copy).then_inc(feat_copied, 1)
                for r in plan.rows_at(s, 4, 4):
                    p, m = plan.rows[r]
                    i = r - 4 * NB
                    act.wait_ge(out_ready, i + 1)
                    act.dma_start(out_v[:, m], out_rows[i % 2][:, :, :]).then_inc(out_stored[i % 2], 16)
            for i in range(2):
                act.wait_ge(out_stored[i], 16 * NB // 2)

        @block.vector
        def _(dve):
            chain = Chain(dve, dve_step)
            stt = nc.vector.scalar_tensor_tensor

            def centre(row, v, m, out):
                chain.step(nc.vector.tensor_reduce(total[:, of(m)], v, AX.X, ALU.add))
                stt(out, over_features(total[:, of(m)]), -1.0 / D, v, ALU.mult, ALU.add).then_inc(centred, 1)

            def variance(row, squares, m):
                dve.wait_ge(squared, LN_NO[row] + 1)
                chain.step(nc.vector.tensor_reduce(rstd[:, of(m)], squares, AX.X, ALU.add))
                nc.vector.tensor_scalar(rstd[:, of(m)], rstd[:, of(m)], 1.0 / D, EPS, ALU.mult, ALU.add).then_inc(var_ready, 1)

            def relu_norm(row, c, m, out):
                dve.wait_ge(pow_ready, LN_NO[row] + 1)
                return stt(out, c, 0.0, over_features(rstd[:, of(m)]), ALU.max, ALU.mult)

            def sum_rows(g, m):
                dve.wait_ge(raw_in[m], g * 16 + 16)
                out = deg_part[:, of(m), g] if isinstance(g, int) else \
                    deg_part[:, of(m), bass.ds(g, 1)].rearrange("p a g -> p (a g)")
                nc.vector.tensor_reduce(out, raw[:, m], AX.X, ALU.add).then_inc(deg_summed, 1)

            dve.wait_ge(x_in, 16)
            for i in range(NB + 4):
                if i < NB:
                    centre(("start", i), X[:, of(i), :], i, R[:, of(i), :])
                if 0 <= i - 1 < NB:
                    variance(("start", i - 1), sq[(i - 1) % 2][:, :, :], i - 1)
                if 0 <= i - 2 < NB:
                    m = i - 2
                    chain.step(relu_norm(("start", m), R[:, of(m), :], m, R[:, of(m), :]))
                    if m == 0:
                        dve.wait_ge(early_in, 16 * 6)
                        chain.step(nc.vector.tensor_tensor(par[:, 0:1], par[:, 0:1], par[:, 1:2], ALU.mult))
                        chain.step(nc.vector.tensor_tensor(par[:, 2:3], par[:, 2:3], par[:, 3:4], ALU.mult))
                    nc.vector.tensor_tensor(S[:, of(m), :], R[:, of(m), :], over_features(diag[:, of(m)]),
                                            ALU.mult).then_inc(ego_ready, 1)
                if 0 <= i - 4 < NB:
                    m = i - 4
                    dve.wait_ge(ego_mult, m + 1)
                    stt(E[:, of(m), :], ego_product, par[:, 0:1] if m * B < U else par[:, 2:3], R[:, of(m), :],
                        ALU.mult, ALU.add).then_inc(e_ready, 1)
                    if m < NB - 1:
                        sum_rows(0, m)

            def take_t_rest(g):
                dve.wait_ge(t_high, g + 1)
                nc.vector.tensor_tensor(t_cur[:, :, D:2 * D], aux_rows[1], t_cur[:, :, 0:D].bitcast(F32),
                                        ALU.subtract).then_inc(t_ready, 1)

            def take_low(g, m):
                dve.wait_ge(high_ready, g * NB + (m + 1))
                nc.vector.tensor_tensor(low[m % 2][:, :, :], whole[m % 2][:, :, :],
                                        high[m % 2][:, :, :].bitcast(F32), ALU.subtract).then_inc(low_ready, 1)

            def add_h(g, m):
                dve.wait_ge(used, g * NB + (m + 1))
                if isinstance(g, int) and g == 0:
                    ins = nc.vector.tensor_copy(h_acc[:, m, :], acc[m % 2][:, :])
                else:
                    ins = nc.vector.tensor_tensor(h_acc[:, m, :], acc[m % 2][:, :], h_acc[:, m, :], ALU.add)
                ins.then_inc(h_added, 1)

            def end_of_layer(i):
                if 0 <= i - 1 < NB:
                    variance(("h", i - 1), sq[(i - 1) % 2][:, :, :], i - 1)
                if 0 <= i - 2 < NB:
                    m = i - 2
                    dve.wait_ge(x_ready, m + 1)
                    centre(("x", m), X[:, of(m), :], m, E[:, of(m), :])
                if 0 <= i - 4 < NB:
                    variance(("x", i - 4), cen[(i - 4) % 2][:, :, :], i - 4)
                if 0 <= i - 5 < NB:
                    m = i - 5
                    relu_norm(("x", m), E[:, of(m), :], m, R[:, of(m), :]).then_inc(rows_ready, 1)
                if 0 <= i - 7 < NB:
                    m = i - 7
                    dve.wait_ge(upper_ready, m + 1)
                    nc.vector.tensor_tensor(feats[0][:, of(m), D:2 * D], R[:, of(m), :],
                                            feats[0][:, of(m), 0:D].bitcast(F32), ALU.subtract).then_inc(feats_ready, 1)

            def group(g, followed=True):
                take_t_rest(g)
                for m in range(NB):
                    if m + 1 < NB or followed:
                        take_low(g, m + 1)
                    if m == 0 and not (isinstance(g, int) and g == 0):
                        dve.wait_ge(h_added, g * NB)
                    add_h(g, m)
                    if m == 0:
                        sum_rows(g, NB - 1)
                    elif followed:
                        sum_rows(g + 1, m - 1)
                    if not followed and m >= 1:
                        end_of_layer(m - 1)

            take_low(0, 0)
            group(0)
            with dve.Fori(1, NB - 1) as g:
                group(g)
            dve.wait_ge(late_in, 16 * 8)
            group(NB - 1, followed=False)
            dve.wait_ge(deg_summed, TOTAL_TILES)
            nc.vector.tensor_reduce(dis[:, :], deg_part[:, :, :], AX.X, ALU.add).then_inc(deg_ready, 1)

            def take_rest(r):
                p, m = plan.rows[r]
                dve.wait_ge(upper_ready, NB + r + 1)
                nc.vector.tensor_tensor(feats[(p + 1) % 2][:, of(m), D:2 * D], MADE[p][:, of(m), :],
                                        feats[(p + 1) % 2][:, of(m), 0:D].bitcast(F32), ALU.subtract).then_inc(feats_ready, 1)

            for s in range(N_STEPS):
                n = plan.step_tile[s]
                if n is not None:
                    slot = n % SLOTS
                    dve.wait_ge(high_ready, TOTAL_TILES + n + 1)
                    nc.vector.tensor_tensor(low[slot][:, :, :], whole[slot][:, :, :], high[slot][:, :, :].bitcast(F32),
                                            ALU.subtract).then_inc(low_ready, 1)
                if NB - 1 + s < END_STAGES:
                    end_of_layer(NB - 1 + s)
                for r in plan.rows_at(s, SPLIT[3], 3):
                    take_rest(r)
                for r in plan.rows_at(s, MAKE[3][1], 3):
                    p, m = plan.rows[r]
                    dve.wait_ge(feat_mult, plan.weigh_no[r] + 1)
                    g = E[:, of(m), :]
                    nc.vector.tensor_tensor(g, weighed, over_nodes(b3), ALU.add).then_inc(mult_read, 1)
                    dve.wait_ge(mult_read, plan.weigh_no[r] + 1)
                    dve.wait_ge(dis_ready, 1)
                    nc.vector.tensor_tensor(g, g, over_features(dis[:, of(m)]), ALU.mult).then_inc(rows_ready, 1)
                for r in plan.rows_at(s, MAKE[3][0], 3):
                    p, m = plan.rows[r]
                    relu_norm((p, m), cen[r % 2][:, :, :], m, R[:, of(m), :]).then_inc(rows_ready, 1)
                for r in plan.rows_at(s, NORM[3], 3):
                    variance(plan.rows[r], sq[r % 2][:, :, :], plan.rows[r][1])
                for r in plan.turns_at(s, 2):
                    p, m = plan.rows[r]
                    if p == 0:
                        dve.wait_ge(feat_mult, plan.weigh_no[r] + 1)
                        nc.vector.tensor_tensor(X[:, of(m), :], weighed, X[:, of(m), :], ALU.add).then_inc(mult_read, 1)
                        dve.wait_ge(mult_read, plan.weigh_no[r] + 1)
                for r in plan.rows_at(s, SPLIT[0], 0):
                    take_rest(r)
                for r in plan.rows_at(s, MAKE[0][0], 0):
                    p, m = plan.rows[r]
                    relu_norm((p, m), cen[r % 2][:, :, :], m, E[:, of(m), :]).then_inc(rows_ready, 1)
                    chain.step(nc.vector.tensor_tensor(X[:, of(m), :], X[:, of(m), :], over_nodes(b2), ALU.add))
                for r in plan.rows_at(s, NORM[0], 0):
                    variance(plan.rows[r], sq[r % 2][:, :, :], plan.rows[r][1])
                for r in plan.rows_at(s, SPLIT[1], 1):
                    m = plan.rows[r][1]
                    dve.wait_ge(upper_ready, NB + r + 1)
                    nc.vector.tensor_tensor(feats[0][:, of(m), D:2 * D], y_part,
                                            feats[0][:, of(m), 0:D].bitcast(F32), ALU.subtract).then_inc(feats_ready, 1)
                    nc.vector.tensor_tensor(X[:, of(m), :], y_weighed, X[:, of(m), :], ALU.add).then_inc(y_read, 1)
                for r in plan.rows_at(s, SPLIT[2], 2):
                    take_rest(r)
                for r in plan.rows_at(s, 2, *range(PASSES)):
                    p, m = plan.rows[r]
                    if p == 1:
                        continue
                    dve.wait_ge(y_rows, r + 1)
                    if p == 0:
                        x = X[:, of(m), :]
                        nc.vector.tensor_tensor(x, aux_rows[0], x, ALU.add).then_inc(y_read, 1)
                        dve.wait_ge(y_read, r + 1)
                        centre((p, m), x, m, cen[r % 2][:, :, :])
                    elif p == 2:
                        v = E[:, of(m), :]
                        stt(v, y_part, 2.0, v, ALU.mult, ALU.subtract).then_inc(rows_ready, 1)
                        nc.vector.tensor_tensor(X[:, of(m), :], y_weighed, X[:, of(m), :], ALU.add).then_inc(y_read, 1)
                    elif p == 3:
                        nc.vector.tensor_tensor(X[:, of(m), :], y_weighed, X[:, of(m), :], ALU.add).then_inc(y_read, 1)
                        dve.wait_ge(y_read, r + 1)
                        centre((p, m), X[:, of(m), :], m, cen[r % 2][:, :, :])
                    else:
                        i = r - 4 * NB
                        o = cen[r % 2][:, :, :]
                        nc.vector.tensor_tensor(o, aux_rows[0], E[:, of(m), :], ALU.add).then_inc(y_read, 1)
                        dve.wait_ge(y_read, r + 1)
                        chain.step(stt(o, o, 0.0, over_features(dis[:, of(m)]), ALU.max, ALU.mult))
                        if i >= 2:
                            dve.wait_ge(out_stored[i % 2], 16 * (i // 2))
                        nc.vector.tensor_tensor(out_rows[i % 2][:, :, :], o, X[:, of(m), :], ALU.add).then_inc(out_ready, 1)
                for r in plan.rows_at(s, 1, *range(PASSES)):
                    p, m = plan.rows[r]
                    dve.wait_ge(multiplied, plan.own_no[plan.last_own[p, m]])
                    if r >= 2:
                        dve.wait_ge(y_rows, r - 1)
                    if (p, m) in DUAL_NO:
                        dve.wait_ge(part_saved, DUAL_NO[p, m] + 1)
                        ins = nc.vector.tensor_tensor(y_sb[r % 2][:, :], own_bank[plan.bank(r)], part[:, m, :], ALU.add)
                    else:
                        ins = nc.vector.tensor_copy(y_sb[r % 2][:, :], own_bank[plan.bank(r)])
                    ins.then_inc(y_saved, 1)

        @block.gpsimd
        def _(pool):
            op = nc.gpsimd
            chain = Chain(pool, pool_step)
            chain.step(op.memset(minus_half[:, :], -0.5))
            chain.step(op.memset(ident[:, :], 0.0))
            chain.step(op.memset(fold[:, :], 0.0))
            op.affine_select(out=ident[:, :], in_=ident[:, :], compare_op=ALU.not_equal, fill=1.0, base=0,
                             pattern=[[-1, P]], channel_multiplier=1).then_inc(made, 1)
            op.affine_select(out=fold[:, :], in_=fold[:, :], compare_op=ALU.not_equal, fill=1.0, base=0,
                             pattern=[[-1, D]], channel_multiplier=1).then_inc(made, 1)
            pool.wait_ge(made, 2)
            op.affine_select(out=fold[:, :], in_=fold[:, :], compare_op=ALU.not_equal, fill=1.0, base=-D,
                             pattern=[[-1, D]], channel_multiplier=1).then_inc(made, 1)

            pool.wait_ge(made, 3)
            op.tensor_scalar(fold_centred[:, :], fold[:, :], -1.0 / D, None, ALU.add).then_inc(made, 1)

            def raise_variances(rows):
                for row in rows:
                    pool.wait_ge(var_ready, LN_NO[row] + 1)
                    v = rstd[:, of(row[1])]
                    op.tensor_tensor(v, v, minus_half[:, 0:SUB], ALU.pow).then_inc(pow_ready, 1)

            raise_variances(LN_START)
            pool.wait_ge(e_ready, NB)
            pool.wait_ge(late_in, 16 * 8)
            chain.step(op.tensor_tensor(X[:, :, :], X[:, :, :], R[:, :, :], ALU.add))
            chain.step(op.tensor_tensor(X[:, :, :], X[:, :, :], bet[:, :].unsqueeze(1).broadcast_to([P, NT, D]), ALU.add))
            chain.step(op.tensor_copy(fold_weigh[:, :, 0:D], fold[:, :].unsqueeze(1).broadcast_to([P, 3, D])))
            chain.step(op.tensor_tensor(w0[:, :], w0[:, :], fold_weigh[0:D, 1, D:2 * D], ALU.subtract))
            chain.step(op.tensor_tensor(fold_weigh[:, 0, D:2 * D], fold_weigh[:, 0, D:2 * D], fold_weigh[:, 2, D:2 * D],
                                        ALU.subtract))
            op.tensor_scalar(fold_weigh[:, 1:3, D:2 * D], fold_weigh[:, 1:3, D:2 * D], 2.0, None, ALU.mult) \
                .then_inc(weights_ready, 1)
            for row in LN_H:
                raise_variances([row])
                if row[0] == "h":
                    m = row[1]
                    e, x = E[:, of(m), :], X[:, of(m), :]
                    pool.wait_ge(pow_ready, LN_NO[row] + 1)
                    chain.step(op.tensor_tensor(e, e, over_features(rstd[:, of(m)]), ALU.mult))
                    chain.step(op.tensor_tensor(e, e, over_nodes(gam), ALU.mult))
                    op.tensor_tensor(x, x, e, ALU.add).then_inc(x_ready, 1)
            pool.wait_ge(deg_ready, 1)
            chain.step(op.tensor_scalar(dis[:, :], dis[:, :], 1.0, None, ALU.add))
            chain.step(op.tensor_scalar(diag[:, :], dis[:, :], 0.0, None, ALU.is_equal))
            chain.step(op.tensor_tensor(dis[:, :], dis[:, :], diag[:, :], ALU.add))
            chain.step(op.tensor_tensor(dis[:, :], dis[:, :], minus_half[:, :], ALU.pow))
            chain.step(op.tensor_scalar(diag[:, :], diag[:, :], -1.0, 1.0, ALU.mult, ALU.add))
            op.tensor_tensor(dis[:, :], dis[:, :], diag[:, :], ALU.mult).then_inc(dis_ready, 1)
            raise_variances(LN_PASS)


_INS = ['x', 'adj', 'L0_gnn_W_u', 'L0_gnn_diag_u', 'L0_gnn_par_u', 'L0_gnn_W_i', 'L0_gnn_diag_i', 'L0_gnn_par_i',
        'L0_gnn_ln_gamma', 'L0_gnn_ln_beta', 'L2_gnn_weights', 'L2_gnn_bias', 'L3_gnn_W', 'L3_gnn_b']


def kernel(**inputs):
    import numpy as _np
    import concourse.bacc as _bacc
    from concourse import mybir as _mybir
    from concourse.bass_utils import run_bass_kernel_spmd as _run

    nc = _bacc.Bacc("TRN2", target_bir_lowering=False, num_devices=1)
    arrays, args = {}, []
    for name in _INS:
        a = _np.ascontiguousarray(inputs[name])
        arrays[f"in_{name}_dram"] = a
        args.append(nc.dram_tensor(f"in_{name}_dram", a.shape, _mybir.dt.from_np(a.dtype), kind="ExternalInput").ap())
    out = nc.dram_tensor("out_dram", (N, D), _mybir.dt.float32, kind="ExternalOutput").ap()
    gnn_stack(nc, *args, out)
    r = _run(nc, [arrays], core_ids=[0])
    return r.results[0]["out_dram"]
```
